# Optimizing a Trainium2 kernel written in Bass

```python
import numpy as np
import jax
import jax.numpy as jnp

def _softmax(x, axis=-1):
    return jax.nn.softmax(x, axis=axis)

def _gelu(x):
    return jax.nn.gelu(x, approximate=True)

def _silu(x):
    return jax.nn.silu(x)

def _sigmoid(x):
    return jax.nn.sigmoid(x)

def _layernorm(x, axis=-1, eps=1e-05):
    m = jnp.mean(x, axis=axis, keepdims=True)
    v = jnp.var(x, axis=axis, keepdims=True)
    return (x - m) / jnp.sqrt(v + eps)

def _scatter_add(tgt, idx, src, axis=0):
    return tgt.at[idx].add(src)

def _segment_sum(src, seg, n):
    return jax.ops.segment_sum(src, seg, n)
kernel_name = 'mk_xattn_ffn_d1_seqx_r4_6feb5a'

def setup_inputs(seed: int=0):
    np.random.seed(seed)
    _w = jnp.asarray

    def _rec_inputs():
        import jax
        import jax.numpy as jnp
        _rk = jax.random.key(seed)
        x = -0.0003929 + 0.9999 * jax.random.normal(jax.random.fold_in(_rk, 1), (4, 1024, 256), jnp.float32)
        _lenS = 1024 - jax.random.randint(jax.random.fold_in(_rk, 7), (4,), 0, max(1, 1024 // 4) + 1, jnp.int32)
        _lenS2 = 154 - jax.random.randint(jax.random.fold_in(_rk, 8), (4,), 0, max(1, 154 // 4) + 1, jnp.int32)
        _ctx_1024P = jax.random.normal(jax.random.fold_in(_rk, 11), (4, 16, 256), jnp.float32)
        _ctx_1024c = jax.random.dirichlet(jax.random.fold_in(_rk, 511), 0.3 * jnp.ones((16,), jnp.float32), (4, 154))
        _ctx_1024t = jnp.einsum('bsk,bkd->bsd', _ctx_1024c, _ctx_1024P)
        _ctx_1024t = _ctx_1024t * jax.lax.rsqrt(jnp.mean(jnp.square(_ctx_1024t)) + 1e-12) * 0.953939
        ctx_1024 = 2.81802e-05 + 1.00001 * (_ctx_1024t + 0.3 * jax.random.normal(jax.random.fold_in(_rk, 611), (4, 154, 256), jnp.float32))
        _validS = jnp.arange(1024)[None, :] < _lenS[:, None]
        _validS2 = jnp.arange(154)[None, :] < _lenS2[:, None]
        _causal = jnp.tril(jnp.ones((1024, 1024), dtype=bool))
        mask_SxS2_bk0 = jnp.logical_not(jnp.broadcast_to(_validS2[0:1, :], (1024, 154)))
        return (x, ctx_1024, mask_SxS2_bk0)
    x, ctx_1024, mask_SxS2_bk0 = _rec_inputs()

    def _L0_xattn_setup():
        import jax, jax.numpy as jnp
        import numpy as np
        B, S, D = (8, 512, 256)
        key = jax.random.key(seed)
        ks = jax.random.split(key, 9)
        scale = 1.0 / np.sqrt(D)
        inp = {'query': jax.random.normal(ks[0], (B, S, D), dtype=jnp.float32), 'key': jax.random.normal(ks[1], (B, S, D), dtype=jnp.float32), 'value': jax.random.normal(ks[2], (B, S, D), dtype=jnp.float32), 'mask': jnp.tril(jnp.ones((S, S), dtype=bool)), 'Wq': jax.random.normal(ks[3], (D, D), dtype=jnp.float32) * scale, 'bq': jax.random.normal(ks[4], (D,), dtype=jnp.float32) * 0.02, 'Wk': jax.random.normal(ks[5], (D, D), dtype=jnp.float32) * scale, 'bk': jax.random.normal(ks[6], (D,), dtype=jnp.float32) * 0.02, 'Wv': jax.random.normal(ks[7], (D, D), dtype=jnp.float32) * scale, 'bv': jax.random.normal(ks[8], (D,), dtype=jnp.float32) * 0.02}
        return inp
    _L0_xattn_all = _L0_xattn_setup()
    _L0_xattn_in = {k: v for k, v in _L0_xattn_all.items() if k in ('Wq', 'bq', 'Wk', 'bk', 'Wv', 'bv')}
    del _L0_xattn_all

    def _L0_ffn_setup():
        import jax, jax.numpy as jnp
        import numpy as np
        B, L, D = (4, 256, 256)
        E, H, K = (16, 128, 8)
        EPS = 1e-12

        def _l2norm(v, axis=-1):
            n = jnp.sqrt(jnp.sum(v * v, axis=axis, keepdims=True))
            return v / jnp.maximum(n, EPS)
        if __name__ == '__main__':
            out = reference(**setup_inputs())
            print(out.shape)
        key = jax.random.key(seed)
        ks = jax.random.split(key, 8)
        s = lambda fan_in: 1.0 / np.sqrt(fan_in)
        return {'x': jax.random.normal(ks[0], (B, L, D), jnp.float32), 'gate_w': jax.random.normal(ks[1], (E, D), jnp.float32) * s(D), 'w_gate': jax.random.normal(ks[2], (E, D, H), jnp.float32) * s(D), 'w_up': jax.random.normal(ks[3], (E, D, H), jnp.float32) * s(D), 'w_down': jax.random.normal(ks[4], (E, H, D), jnp.float32) * s(H), 'sw_gate': jax.random.normal(ks[5], (D, H), jnp.float32) * s(D), 'sw_up': jax.random.normal(ks[6], (D, H), jnp.float32) * s(D), 'sw_down': jax.random.normal(ks[7], (H, D), jnp.float32) * s(H)}
    _L0_ffn_all = _L0_ffn_setup()
    _L0_ffn_in = {k: v for k, v in _L0_ffn_all.items() if k in ('gate_w', 'w_gate', 'w_up', 'w_down', 'sw_gate', 'sw_up', 'sw_down')}
    del _L0_ffn_all
    return {'x': x, 'ctx_1024': ctx_1024, 'mask_SxS2_bk0': mask_SxS2_bk0, 'L0_xattn_Wq': _L0_xattn_in['Wq'], 'L0_xattn_bq': _L0_xattn_in['bq'], 'L0_xattn_Wk': _L0_xattn_in['Wk'], 'L0_xattn_bk': _L0_xattn_in['bk'], 'L0_xattn_Wv': _L0_xattn_in['Wv'], 'L0_xattn_bv': _L0_xattn_in['bv'], 'L0_ffn_gate_w': _L0_ffn_in['gate_w'], 'L0_ffn_w_gate': _L0_ffn_in['w_gate'], 'L0_ffn_w_up': _L0_ffn_in['w_up'], 'L0_ffn_w_down': _L0_ffn_in['w_down'], 'L0_ffn_sw_gate': _L0_ffn_in['sw_gate'], 'L0_ffn_sw_up': _L0_ffn_in['sw_up'], 'L0_ffn_sw_down': _L0_ffn_in['sw_down']}

def reference(x, ctx_1024, mask_SxS2_bk0, L0_xattn_Wq, L0_xattn_bq, L0_xattn_Wk, L0_xattn_bk, L0_xattn_Wv, L0_xattn_bv, L0_ffn_gate_w, L0_ffn_w_gate, L0_ffn_w_up, L0_ffn_w_down, L0_ffn_sw_gate, L0_ffn_sw_up, L0_ffn_sw_down):
    import jax
    import jax.numpy as jnp

    def _L0_xattn_ref(query, key, value, mask, Wq, bq, Wk, bk, Wv, bv):
        import jax, jax.numpy as jnp
        import numpy as np
        B, S, D = (8, 512, 256)
        dk = Wq.shape[1]
        q = jnp.einsum('bsd,de->bse', query, Wq) + bq
        k = jnp.einsum('bsd,de->bse', key, Wk) + bk
        v = jnp.einsum('bsd,de->bse', value, Wv) + bv
        scores = jnp.einsum('bqd,bkd->bqk', q, k) / jnp.sqrt(jnp.asarray(dk, q.dtype))
        scores = jnp.where(mask, scores, jnp.asarray(-jnp.inf, scores.dtype))
        attn = jax.nn.softmax(scores, axis=-1)
        return jnp.einsum('bqk,bkd->bqd', attn, v)

    def _L0_ffn_ref(x, gate_w, w_gate, w_up, w_down, sw_gate, sw_up, sw_down):
        import jax, jax.numpy as jnp
        import numpy as np
        B, L, D = (4, 256, 256)
        E, H, K = (16, 128, 8)
        EPS = 1e-12

        def _l2norm(v, axis=-1):
            n = jnp.sqrt(jnp.sum(v * v, axis=axis, keepdims=True))
            return v / jnp.maximum(n, EPS)
        if __name__ == '__main__':
            out = reference(**setup_inputs())
            print(out.shape)
        b, l, d = x.shape
        xf = x.reshape(-1, d)
        logits = _l2norm(xf) @ _l2norm(gate_w).T
        scores = jax.nn.sigmoid(logits)
        topk_scores, topk_idx = jax.lax.top_k(scores, K)
        topk_w = topk_scores / jnp.sum(topk_scores, axis=-1, keepdims=True)
        combine = jnp.sum(jax.nn.one_hot(topk_idx, E, dtype=xf.dtype) * topk_w[..., None], axis=1)
        g = jnp.einsum('nd,edh->neh', xf, w_gate)
        u = jnp.einsum('nd,edh->neh', xf, w_up)
        y = jnp.einsum('neh,ehd->ned', jax.nn.silu(g) * u, w_down)
        routed = jnp.einsum('ned,ne->nd', y, combine)
        shared = jax.nn.silu(xf @ sw_gate) * (xf @ sw_up) @ sw_down
        return (routed + shared).reshape(b, l, d)
    x = x + _L0_xattn_ref(_layernorm(x, axis=-1), ctx_1024, ctx_1024, mask_SxS2_bk0, L0_xattn_Wq, L0_xattn_bq, L0_xattn_Wk, L0_xattn_bk, L0_xattn_Wv, L0_xattn_bv)
    x = x + _L0_ffn_ref(_layernorm(x, axis=-1), L0_ffn_gate_w, L0_ffn_w_gate, L0_ffn_w_up, L0_ffn_w_down, L0_ffn_sw_gate, L0_ffn_sw_up, L0_ffn_sw_down)
    return x

_drawn_inputs = setup_inputs


def setup_inputs(seed=0):
    import zlib

    import numpy as np

    out = dict(_drawn_inputs(seed))
    spreads = {}
    factors = {'L0_xattn_bq': 5.549, 'L0_xattn_bk': 8.0}
    for name, (base, spread) in spreads.items():
        noise = np.random.default_rng([zlib.crc32(name.encode()), seed]).standard_normal(out[name].shape)
        drawn = base * np.exp(spread * noise) if base else spread * noise
        out[name] = jnp.asarray(drawn.astype(out[name].dtype))
    for name, factor in factors.items():
        out[name] = (out[name] * factor).astype(out[name].dtype)
    return out
```

```python
from contextlib import ExitStack

import concourse.bass as bass
from concourse import mybir

ALU = mybir.AluOpType
ACT = mybir.ActivationFunctionType
AX_X = mybir.AxisListType.X
F32 = mybir.dt.float32
F32R = mybir.dt.float32r
U32 = mybir.dt.uint32
U8 = mybir.dt.uint8

P = 128
LN_EPS = 1e-5
NORM_EPS = 1e-12
MASKED = -3e38
HI, LO = 0, 1


def xattn_moe_kernel(nc, x, ctx, mask, Wq, bq, Wk, bk, Wv, bv, gate_w, w_gate, w_up, w_down,
                     sw_gate, sw_up, sw_down, out):
    B, S, D = x.shape
    KEYS = ctx.shape[1]
    E, _, H = w_gate.shape
    TOK = 512
    TILES = TOK // P
    CHUNKS = B * S // TOK
    KD = D // P
    NE = E + 1
    TAIL = KEYS - P
    STACK = 96
    CKEYS = B * KEYS
    CT = -(-CKEYS // P)
    HALF = CKEYS // 2
    WCOLS = 2 * KD * H + D
    UP0, DN0 = KD * H, 2 * KD * H
    SCALE = float(D) ** -0.5
    assert S == 2 * TOK and KD == 2 and H == P and 0 < TAIL <= 32 and E % 4 == 0 and NE % 2 == 1
    assert nc is not None and HALF <= 512

    x_rows = x.rearrange("b s d -> (b s) d").rearrange("(c j p) d -> c p j d", p=P, j=TILES)
    out_rows = out.rearrange("b s d -> (b s) d").rearrange("(c j p) d -> c p j d", p=P, j=TILES)
    ctx_rows = ctx.rearrange("b s d -> (b s) d")

    with ExitStack() as stack:
        def sb(name, shape, dt=F32):
            return stack.enter_context(nc.sbuf_tensor(name, shape, dt))

        def sem(name):
            return stack.enter_context(nc.semaphore(name))

        W = sb("W", [P, NE, 2, WCOLS], F32R)
        A = sb("A", [P, B, 2, KD, KEYS], F32R)
        Brow = sb("Brow", [2, CKEYS], F32R)
        V = sb("V", [P, B, 2, D], F32R)
        Vtail = sb("Vtail", [STACK, B, D], F32R)
        G = sb("G", [P, KD, 2 * E], F32R)
        keep = sb("keep", [P, S // P, KEYS])
        ident = sb("ident", [P, P])
        ones2 = sb("ones2", [2, P], F32R)
        minus_half = sb("minus_half", [P, TILES])
        xin = sb("xin", [P, TILES, D])
        x2 = sb("x2", [P, 2, TILES, D])
        xn = sb("xn", [P, TILES, D])
        xT = sb("xT", [P, 2, 2, KD, TOK], F32R)
        att = sb("att", [P, TILES, KEYS])
        ptail = sb("ptail", [STACK, TOK], F32R)
        stats = sb("stats", [P, TILES, 6])
        meanvar = sb("meanvar", [P, TILES, 2])
        small = sb("small", [P, 12, TILES])
        var_eps, rstd, nmax, esum, rsum, rsq, nsq, inorm, ssum, srec = (small[:, i, :] for i in range(10))
        route = sb("route", [P, 4, TILES, E])
        z, score, rest, cw = (route[:, i] for i in range(4))
        top8 = sb("top8", [P, TILES, 8])
        cT = sb("cT", [P, TOK])
        crow = sb("crow", [P, E // 4, TOK])
        hidden = sb("hidden", [P, 3, 2, TOK])
        ew = hidden[:, 0]
        h = hidden[:, 1]
        cb = hidden[:, 2]
        hs = sb("hs", [P, 2, 2, TOK], F32R)
        ysb = sb("ysb", [P, KD, TOK])
        STAGES = 3
        stage = sb("stage", [P, STAGES, WCOLS])
        hidden_flat = hidden[:].rearrange("p a b t -> p (a b t)")
        crow_flat = crow[:].rearrange("p r t -> p (r t)")
        ctx_in = crow_flat[:, 0:CT * D].rearrange("p (t d) -> p t d", t=CT)
        wk_in = x2[:, 1, 0:KD, :]
        wq_in = x2[:, 0, 0:KD, :]
        wv_in = x2[:, 1, KD:2 * KD, :]
        ctxT = hidden_flat[:, 0:KD * CKEYS].rearrange("p (k c) -> p k c", k=KD)
        wqT = ysb[:, :, 0:D]
        KT = hidden_flat[:, KD * CKEYS:2 * KD * CKEYS].rearrange("p (k c) -> p k c", k=KD)
        bk_col = sb("bk_col", [P, KD])
        bq_col = sb("bq_col", [P, KD])
        bq2 = sb("bq2", [P, KD, 2])
        bv_row = sb("bv_row", [1, D])
        ones1 = sb("ones1", [2, P])
        brow_f = crow_flat[0:2, CT * D:CT * D + CKEYS]
        brow_hi = sb("brow_hi", [2, CKEYS], F32R)
        lo_row = sb("lo_row", [2, 1])
        gw_in = sb("gw_in", [E, D])
        gw_n = sb("gw_n", [E, D])
        gsq = sb("gsq", [E, 4])
        mask_in = cT[:].bitcast(U8)[:, 0:S // P * KEYS].rearrange("p (t k) -> p t k", k=KEYS)
        zero_keys = att[:, 0, :]

        def bank(name):
            return stack.enter_context(nc.psum_tensor(name, [P, 512], F32))

        gate_ps = [bank(f"gate_ps{i}") for i in range(2)]
        up_ps = [bank(f"up_ps{i}") for i in range(2)]
        y_ps = [bank(f"y_ps{i}") for i in range(2)]
        f_ps = [bank(f"f_ps{i}") for i in range(2)]

        ctx_loaded, w_in_loaded, small_loaded, mask_loaded, x_loaded, stored, crow_loaded = (
            sem(n) for n in ("ctx_loaded", "w_in_loaded", "small_loaded", "mask_loaded", "x_loaded", "stored",
                             "crow_loaded"))
        staged = [sem(f"staged{i}") for i in range(STAGES)]
        (consts_set, ctx_turned, ctxT_read, wq_turned, wqT_read, kt_made, kt_read, a_made, a_hi, a_lo, brow_made,
         brow_scaled, brow_split, v_made, v_hi, v_lo, gate_summed, gate_inv, gate_scaled, gate_turned, gate_split,
         keep_set, pads_set, w_hi, w_lo) = (
            sem(n) for n in ("consts_set", "ctx_turned", "ctxT_read", "wq_turned", "wqT_read", "kt_made", "kt_read",
                             "a_made", "a_hi", "a_lo", "brow_made", "brow_scaled", "brow_split", "v_made", "v_hi", "v_lo",
                             "gate_summed", "gate_inv", "gate_scaled", "gate_turned", "gate_split", "keep_set",
                             "pads_set", "w_hi", "w_lo"))
        (ln1_stats, ln1_rstd, ln1_done, t1_turned, t1_hi, t1_lo, scored, maxed, exped, rsummed, p_turned, p_hi, p_lo,
         attended, x2_made, ln2_stats, ln2_rstd, inv_norms, ln2_done, t2_turned, t2_hi, t2_lo, routed_z, z_summed,
         tanh_z, scores_set, topped, rest_set, picked, combined, c_turned, c_read, bn_step, pool_step) = (
            sem(n) for n in ("ln1_stats", "ln1_rstd", "ln1_done", "t1_turned", "t1_hi", "t1_lo", "scored", "maxed",
                             "exped", "rsummed", "p_turned", "p_hi", "p_lo", "attended", "x2_made", "ln2_stats",
                             "ln2_rstd", "inv_norms", "ln2_done", "t2_turned", "t2_hi", "t2_lo", "routed_z",
                             "z_summed", "tanh_z", "scores_set", "topped", "rest_set", "picked", "combined",
                             "c_turned", "c_read", "bn_step", "pool_step"))
        (gate_done, up_done, tanh_done, silu_done, prod_done, c_spread, h_done, h_hi, h_lo, down_done, y_read,
         y_turned, y_added) = (
            sem(n) for n in ("gate_done", "up_done", "tanh_done", "silu_done", "prod_done", "c_spread", "h_done",
                             "h_hi", "h_lo", "down_done", "y_read", "y_turned", "y_added"))

        FREE = 2

        def upto(b, hf, per, k):
            return b * (2 * per) + (per * hf + k)

        def first_chunk(b, hf):
            return isinstance(b, int) and b == 0 and hf == 0

        def wait_apart(eng, *waits):
            counts = [n if isinstance(n, int) else eng.to_reg(n) for _, n in waits]
            eng.wait_ge(consts_set, 1)
            for (what, _), n in zip(waits, counts):
                if not isinstance(n, int) or n > 0:
                    eng.wait_ge(what, n)

        def slot(hf, e):
            return (NE * hf + e) % 2

        def nxt(hf, e):
            return (hf, e) if e < NE else (hf + 1, e - NE)

        block = stack.enter_context(nc.Block())

        @block.sync
        def _(sp):
            sp.sem_inc(stored, 16 * FREE)
            sp.dma_start(ctx_in[:, 0:CT - 1, :], ctx_rows[0:(CT - 1) * P, :].rearrange("(t p) d -> p t d", p=P)) \
                .then_inc(ctx_loaded, 16)
            sp.dma_start(ctx_in[0:CKEYS - (CT - 1) * P, CT - 1, :], ctx_rows[(CT - 1) * P:CKEYS, :]) \
                .then_inc(ctx_loaded, 16)
            sp.dma_start(xin[:], x_rows[0]).then_inc(x_loaded, 16)
            for t, w in ((wk_in[:], Wk), (wq_in, Wq), (wv_in, Wv)):
                sp.dma_start(t, w.rearrange("(k p) e -> p k e", p=P)).then_inc(w_in_loaded, 16)
            sp.dma_start(bk_col[:], bk.rearrange("(k p) -> p k", p=P), allow_slow_non_contiguous=True) \
                .then_inc(small_loaded, 16)
            sp.dma_start(bq_col[:], bq.rearrange("(k p) -> p k", p=P), allow_slow_non_contiguous=True) \
                .then_inc(small_loaded, 16)
            sp.dma_start(bv_row[:], bv.rearrange("(a d) -> a d", a=1)).then_inc(small_loaded, 16)
            sp.dma_start(gw_in[:], gate_w).then_inc(small_loaded, 16)
            sp.dma_start(mask_in[:], mask.rearrange("(t p) k -> p t k", p=P)).then_inc(mask_loaded, 16)
            for e in range(NE):
                if e >= STAGES:
                    sp.wait_ge(w_hi, e - STAGES + 1)
                    sp.wait_ge(w_lo, e - STAGES + 1)
                g, u, d = (sw_gate, sw_up, sw_down) if e == 0 else (w_gate[e - 1], w_up[e - 1], w_down[e - 1])
                s = stage[:, e % STAGES, :]
                sp.dma_start(s[:, 0:UP0].rearrange("p (k h) -> p k h", k=KD), g.rearrange("(k p) h -> p k h", p=P)) \
                    .then_inc(staged[e % STAGES], 16)
                sp.dma_start(s[:, UP0:DN0].rearrange("p (k h) -> p k h", k=KD), u.rearrange("(k p) h -> p k h", p=P)) \
                    .then_inc(staged[e % STAGES], 16)
                sp.dma_start(s[:, DN0:WCOLS], d).then_inc(staged[e % STAGES], 16)
            sp.wait_ge(x2_made, 2)
            sp.dma_start(xin[:], x_rows[1]).then_inc(x_loaded, 16)

            def chunk(b, hf, load):
                if load:
                    sp.wait_ge(x2_made, upto(b, hf, 2, 4))
                    sp.dma_start(xin[:], x_rows[b * 2 + (hf + 2)]).then_inc(x_loaded, 16)
                sp.wait_ge(y_added, upto(b, hf, 2, 2 + FREE))
                sp.dma_start(out_rows[b * 2 + hf], x2[:, hf]).then_inc(stored, 16)

            with sp.Fori(0, B - 1) as b:
                chunk(b, 0, True)
                chunk(b, 1, True)
            chunk(B - 1, 0, False)
            chunk(B - 1, 1, False)
            sp.wait_ge(stored, 16 * (CHUNKS + FREE))

        @block.tensor
        def _(pe):
            mm = nc.tensor.matmul

            def three_pass(ps, pairs, first, last):
                for i, ((lh, ll), (rh, rl)) in enumerate(pairs):
                    mm(ps, lh, rh, start=first and i == 0, stop=False)
                    mm(ps, lh, rl, start=False, stop=False)
                    ins = mm(ps, ll, rh, start=False, stop=last and i == len(pairs) - 1)
                return ins

            def setup():
                pe.wait_ge(consts_set, 1)
                pe.wait_ge(ctx_loaded, 32)
                for k in range(KD):
                    for t in range(CT):
                        n = min(P, CKEYS - t * P)
                        to = gate_ps[k][:, t * P:t * P + n] if t < 4 else up_ps[k][:, 0:n]
                        ins = nc.tensor.transpose(to, ctx_in[0:n, t, k * P:(k + 1) * P], ident[0:n, 0:n])
                    ins.then_inc(ctx_turned, 1)
                pe.wait_ge(w_in_loaded, 48)
                for m in range(KD):
                    for k in range(KD):
                        ins = nc.tensor.transpose(f_ps[m][:, k * P:(k + 1) * P], wq_in[:, k, m * P:(m + 1) * P],
                                                  ident[:])
                    ins.then_inc(wq_turned, 1)
                pe.wait_ge(ctxT_read, 4)
                for m in range(KD):
                    for n in range(2):
                        to = (y_ps if m == 0 else gate_ps)[n][:, 0:HALF]
                        for k in range(KD):
                            ins = mm(to, wk_in[:, k, m * P:(m + 1) * P], ctxT[:, k, n * HALF:(n + 1) * HALF],
                                     start=k == 0, stop=k == KD - 1)
                        ins.then_inc(kt_made, 1)
                pe.wait_ge(kt_read, 4)
                pe.wait_ge(wqT_read, 2)
                for k in range(KD):
                    for n in range(2):
                        to = (up_ps if k == 0 else f_ps)[n][:, 0:HALF]
                        for m in range(KD):
                            ins = mm(to, wqT[:, m, k * P:(k + 1) * P], KT[:, m, n * HALF:(n + 1) * HALF],
                                     start=m == 0, stop=m == KD - 1)
                        ins.then_inc(a_made, 1)
                pe.wait_ge(consts_set, 2)
                for n in range(2):
                    for m in range(KD):
                        ins = mm(y_ps[n][0:2, 0:HALF], bq2[:, m, :], KT[:, m, n * HALF:(n + 1) * HALF],
                                 start=m == 0, stop=m == KD - 1)
                    ins.then_inc(brow_made, 1)
                pe.wait_ge(small_loaded, 64)
                pe.wait_ge(a_lo, 4)
                for bb in range(B):
                    if bb >= 2:
                        pe.wait_ge(v_hi, 3 * (bb - 1))
                        pe.wait_ge(v_lo, 2 * (bb - 1))
                    for t, (r0, n) in enumerate(((0, P), (P, TAIL))):
                        to = (gate_ps if bb % 2 == 0 else up_ps)[t][0:n, 0:D]
                        for k in range(KD):
                            mm(to, ctxT[:, k, bb * KEYS + r0:bb * KEYS + r0 + n], wv_in[:, k, :], start=k == 0,
                               stop=False)
                        ins = mm(to, ones1[0:1, 0:n], bv_row[0:1, :], start=False, stop=True)
                    ins.then_inc(v_made, 1)
                pe.wait_ge(gate_scaled, 1)
                pe.wait_ge(brow_scaled, 2)
                for k in range(KD):
                    ins = nc.tensor.transpose(y_ps[0][:, k * E:(k + 1) * E], gw_n[:, k * P:(k + 1) * P],
                                              ident[0:E, 0:E])
                ins.then_inc(gate_turned, 1)

            def turn_ln(ready, turned, b, hf):
                pe.wait_ge(ready, upto(b, hf, 1, 1))
                for k in range(KD):
                    for j in range(TILES):
                        ins = nc.tensor.transpose(f_ps[k][:, j * P:(j + 1) * P], xn[:, j, k * P:(k + 1) * P], ident[:])
                    ins.then_inc(turned, 1)

            def turn_x(b, hf):
                if not first_chunk(b, hf):
                    pe.wait_ge(y_added, upto(b, hf - 1, 2, FREE))
                turn_ln(ln1_done, t1_turned, b, hf)

            def scores(b, hf):
                pe.wait_ge(t1_hi, upto(b, hf, 2, 2))
                pe.wait_ge(t1_lo, upto(b, hf, 2, 2))
                par, bi = hf % 2, b + hf // 2
                for j in range(TILES):
                    to = f_ps[j // 2][:, (j % 2) * D:(j % 2) * D + KEYS]
                    mm(to, ones2[:], Brow[:, bass.ds(bi * KEYS, KEYS)], start=True, stop=False)
                    c = slice(j * P, (j + 1) * P)
                    ins = three_pass(to, [((xT[:, par, HI, k, c], xT[:, par, LO, k, c]),
                                           (A[:, bi, HI, k, :], A[:, bi, LO, k, :])) for k in range(KD)],
                                     first=False, last=True)
                    if j % 2:
                        ins.then_inc(scored, 1)

            def turn_p(b, hf):
                pe.wait_ge(exped, upto(b, hf, TILES, TILES))
                for q, (c0, n) in enumerate(((0, P), (P, TAIL))):
                    for j in range(TILES):
                        ins = nc.tensor.transpose(f_ps[q][0:n, j * P:(j + 1) * P], att[:, j, c0:c0 + n], ident[:])
                    ins.then_inc(p_turned, 1)

            def attend(b, hf):
                pe.wait_ge(p_hi, upto(b, hf, 3, 3))
                pe.wait_ge(p_lo, upto(b, hf, 2, 2))
                par, bi = hf % 2, b + hf // 2
                for j in range(TILES):
                    to = f_ps[j // 2][:, (j % 2) * D:(j % 2 + 1) * D]
                    c = slice(j * P, (j + 1) * P)
                    three_pass(to, [((xT[:, par, HI, 0, c], xT[:, par, LO, 0, c]), (V[:, bi, HI, :], V[:, bi, LO, :]))],
                               first=True, last=False)
                    ins = mm(to, ptail[:, c], Vtail[:, bi, :], start=False, stop=True)
                    if j % 2:
                        ins.then_inc(attended, 1)

            def logits(b, hf):
                pe.wait_ge(t2_hi, upto(b, hf, 2, 2))
                pe.wait_ge(t2_lo, upto(b, hf, 2, 2))
                par = hf % 2
                for j in range(TILES):
                    o, c = j * 2 * E, slice(j * P, (j + 1) * P)
                    for k in range(KD):
                        mm(f_ps[0][:, o:o + 2 * E], xT[:, par, HI, k, c], G[:, k, :], start=k == 0, stop=False)
                    for k in range(KD):
                        ins = mm(f_ps[0][:, o:o + E], xT[:, par, LO, k, c], G[:, k, 0:E], start=False,
                                 stop=k == KD - 1)
                ins.then_inc(routed_z, 1)

            def turn_c(b, hf):
                pe.wait_ge(combined, upto(b, hf, 1, 1))
                for j in range(TILES):
                    ins = nc.tensor.transpose(f_ps[1][0:E, j * P:(j + 1) * P], cw[:, j, :], ident[:])
                ins.then_inc(c_turned, 1)

            def gate_up(b, hf, e):
                hf, e = nxt(hf, e)
                i, par = slot(hf, e), hf % 2
                if e == 0:
                    pe.wait_ge(t2_hi, upto(b, hf, 2, 2))
                    pe.wait_ge(t2_lo, upto(b, hf, 2, 2))
                if hf == 0:
                    pe.wait_ge(w_hi, e + 1)
                    pe.wait_ge(w_lo, e + 1)
                for ps, col, free, done in ((gate_ps, 0, silu_done, gate_done), (up_ps, UP0, prod_done, up_done)):
                    pe.wait_ge(free, upto(b, hf, NE, e - 1 + FREE))
                    ins = three_pass(ps[i][:], [((W[:, e, HI, col + k * H:col + (k + 1) * H],
                                                  W[:, e, LO, col + k * H:col + (k + 1) * H]),
                                                 (xT[:, par, HI, k, :], xT[:, par, LO, k, :])) for k in range(KD)],
                                     first=True, last=True)
                    ins.then_inc(done, 1)

            def down(b, hf, e):
                i = slot(hf, e)
                pe.wait_ge(h_hi, upto(b, hf, NE, e + 1 + FREE))
                pe.wait_ge(h_lo, upto(b, hf, NE, e + 1 + FREE))
                if e == 0:
                    pe.wait_ge(y_read, upto(b, hf, 2, FREE))
                for m in range(KD):
                    col = DN0 + m * P
                    ins = three_pass(y_ps[m][:], [((W[:, e, HI, col:col + P], W[:, e, LO, col:col + P]),
                                                   (hs[:, i, HI, :], hs[:, i, LO, :]))],
                                     first=e == 0, last=e == NE - 1)
                ins.then_inc(down_done, 1)

            def turn_y(b, hf, front):
                pe.wait_ge(y_read, upto(b, hf, 2, 2 + FREE))
                if front:
                    pe.wait_ge(c_read, upto(b, hf, 1, 2))
                else:
                    pe.wait_ge(y_added, upto(b, hf, 2, FREE))
                for j in range(TILES):
                    for m in range(KD):
                        ins = nc.tensor.transpose(f_ps[j // 2][:, (j % 2) * D + m * P:(j % 2) * D + (m + 1) * P],
                                                  ysb[:, m, j * P:(j + 1) * P], ident[:])
                    if j % 2:
                        ins.then_inc(y_turned, 1)

            def chunk(b, hf, front, last):
                for s in range(NE):
                    down(b, hf, s)
                    if s + 3 < NE or not last:
                        gate_up(b, hf, s + 3)
                    if front:
                        if s == 1:
                            turn_x(b, hf + 1)
                        if s == 3:
                            scores(b, hf + 1)
                        if s == 6:
                            turn_p(b, hf + 1)
                        if s == 8:
                            attend(b, hf + 1)
                        if s == 11:
                            turn_ln(ln2_done, t2_turned, b, hf + 1)
                        if s == 13:
                            logits(b, hf + 1)
                        if s == 15:
                            turn_c(b, hf + 1)
                turn_y(b, hf, front)

            pe.sem_inc(down_done, FREE)
            pe.sem_inc(y_turned, FREE)
            setup()
            turn_x(0, 0)
            scores(0, 0)
            turn_p(0, 0)
            attend(0, 0)
            turn_ln(ln2_done, t2_turned, 0, 0)
            pe.wait_ge(gate_split, 2)
            pe.wait_ge(v_hi, 3 * B)
            pe.wait_ge(v_lo, 2 * B)
            logits(0, 0)
            turn_c(0, 0)
            for e in range(3):
                gate_up(0, 0, e)
            with pe.Fori(0, B - 1) as b:
                chunk(b, 0, True, False)
                chunk(b, 1, True, False)
            chunk(B - 1, 0, True, False)
            chunk(B - 1, 1, False, True)

        @block.scalar
        def _(act):
            af = nc.scalar.activation

            def setup():
                for k in range(KD):
                    act.wait_ge(ctx_turned, k + 1)
                    af(ctxT[:, k, 0:4 * P], gate_ps[k][:], ACT.Copy).then_inc(ctxT_read, 1)
                    af(ctxT[:, k, 4 * P:CKEYS], up_ps[k][:, 0:CKEYS - 4 * P], ACT.Copy).then_inc(ctxT_read, 1)
                act.wait_ge(small_loaded, 64)
                for m in range(KD):
                    for n in range(2):
                        act.wait_ge(kt_made, 2 * m + n + 1)
                        af(KT[:, m, n * HALF:(n + 1) * HALF], (y_ps if m == 0 else gate_ps)[n][:, 0:HALF],
                           ACT.Identity, bias=bk_col[:, m:m + 1]).then_inc(kt_read, 1)
                for k in range(KD):
                    for n in range(2):
                        act.wait_ge(a_made, 2 * k + n + 1)
                        af(A[:, 2 * n:2 * n + 2, HI, k, :],
                           (up_ps if k == 0 else f_ps)[n][:, 0:HALF].rearrange("p (b q) -> p b q", b=2),
                           ACT.Copy, scale=SCALE).then_inc(a_hi, 1)
                for n in range(2):
                    act.wait_ge(brow_made, n + 1)
                    af(brow_f[:, n * HALF:(n + 1) * HALF], y_ps[n][0:2, 0:HALF], ACT.Copy, scale=SCALE) \
                        .then_inc(brow_scaled, 1)
                act.wait_ge(brow_scaled, 2)
                af(brow_hi[:], brow_f[:], ACT.Copy).then_inc(brow_scaled, 1)
                act.wait_ge(pads_set, 1)
                for bb in range(B):
                    act.wait_ge(v_made, bb + 1)
                    ps = gate_ps if bb % 2 == 0 else up_ps
                    af(V[:, bb, HI, :], ps[0][:, 0:D], ACT.Copy).then_inc(v_hi, 1)
                    af(Vtail[0:TAIL, bb, :], ps[1][0:TAIL, 0:D], ACT.Copy).then_inc(v_hi, 1)
                    af(Vtail[32:32 + TAIL, bb, :], ps[1][0:TAIL, 0:D], ACT.Copy).then_inc(v_hi, 1)
                af(gw_n[:], gw_in[:], ACT.Square, accum_out=gsq[:, 0:1]).then_inc(gate_summed, 1)
                act.wait_ge(gate_turned, 1)
                af(G[:, :, 0:E], y_ps[0][:, 0:KD * E].rearrange("p (k e) -> p k e", k=KD), ACT.Copy) \
                    .then_inc(gate_split, 1)

            def split_w(e):
                act.wait_ge(staged[e % STAGES], 48 * (e // STAGES + 1))
                af(W[:, e, HI, :], stage[:, e % STAGES, :], ACT.Copy).then_inc(w_hi, 1)

            def turned_hi(turned, done, b, hf):
                for k in range(KD):
                    act.wait_ge(turned, upto(b, hf, 2, k + 1))
                    af(xT[:, hf % 2, HI, k, :], f_ps[k][:], ACT.Copy).then_inc(done, 1)

            def exps(b, hf):
                for j in range(TILES):
                    act.wait_ge(maxed, upto(b, hf, 2, j // 2 + 1))
                    af(att[:, j, :], att[:, j, :], ACT.Exp, bias=nmax[:, j:j + 1], accum_out=esum[:, j:j + 1]) \
                        .then_inc(exped, 1)

            def probs_hi(b, hf):
                act.wait_ge(p_turned, upto(b, hf, 2, 1))
                af(xT[:, hf % 2, HI, 0, :], f_ps[0][:], ACT.Copy).then_inc(p_hi, 1)
                act.wait_ge(p_turned, upto(b, hf, 2, 2))
                af(ptail[0:TAIL, :], f_ps[1][0:TAIL, :], ACT.Copy).then_inc(p_hi, 1)
                af(ptail[64:64 + TAIL, :], f_ps[1][0:TAIL, :], ACT.Copy).then_inc(p_hi, 1)

            def tanh_scores(b, hf):
                act.wait_ge(z_summed, upto(b, hf, 1, 1))
                act.wait_ge(inv_norms, upto(b, hf, 1, 1))
                for j in range(TILES):
                    ins = af(z[:, j, :], z[:, j, :], ACT.Tanh, scale=inorm[:, j:j + 1])
                ins.then_inc(tanh_z, 1)

            def combine_rows(b, hf):
                act.wait_ge(c_turned, upto(b, hf, 1, 1))
                if not first_chunk(b, hf):
                    act.wait_ge(crow_loaded, upto(b, hf, 64, 0))
                af(cT[0:E, :], f_ps[1][0:E, :], ACT.Copy).then_inc(c_read, 1)
                act.wait_ge(c_read, upto(b, hf, 1, 1))
                if not first_chunk(b, hf):
                    act.wait_ge(c_spread, upto(b, hf, E, 0))
                for g in range(4):
                    act.dma_start(crow[32 * g:32 * g + 1, :, :], cT[4 * g:4 * g + 4, :]).then_inc(crow_loaded, 16)

            def tanh_gate(b, hf, e):
                hf, e = nxt(hf, e)
                i = slot(hf, e)
                act.wait_ge(gate_done, upto(b, hf, NE, e + 1))
                act.wait_ge(h_done, upto(b, hf, NE, e - 1 + FREE))
                af(ew[:, i, :], gate_ps[i][:], ACT.Tanh, scale=0.5).then_inc(tanh_done, 1)

            def hidden_hi(b, hf, e):
                hf, e = nxt(hf, e)
                i = slot(hf, e)
                act.wait_ge(h_done, upto(b, hf, NE, e + 1 + FREE))
                act.wait_ge(down_done, upto(b, hf, NE, e - 1 + FREE))
                af(hs[:, i, HI, :], h[:, i, :], ACT.Copy).then_inc(h_hi, 1)

            def read_y(b, hf):
                act.wait_ge(down_done, upto(b, hf, NE, NE + FREE))
                act.wait_ge(y_turned, upto(b, hf, 2, FREE))
                for m in range(KD):
                    af(ysb[:, m, :], y_ps[m][:], ACT.Copy).then_inc(y_read, 1)

            def chunk(b, hf, front, last):
                for s in range(NE):
                    if s + 2 < NE or not last:
                        tanh_gate(b, hf, s + 2)
                    if s + 1 < NE or not last:
                        hidden_hi(b, hf, s + 1)
                    if front:
                        if s == 2:
                            turned_hi(t1_turned, t1_hi, b, hf + 1)
                        if s == 4:
                            exps(b, hf + 1)
                        if s == 7:
                            probs_hi(b, hf + 1)
                        if s == 12:
                            turned_hi(t2_turned, t2_hi, b, hf + 1)
                        if s == 14:
                            tanh_scores(b, hf + 1)
                        if s == 16:
                            combine_rows(b, hf + 1)
                read_y(b, hf)

            act.sem_inc(h_hi, FREE)
            act.sem_inc(y_read, FREE)
            setup()
            turned_hi(t1_turned, t1_hi, 0, 0)
            exps(0, 0)
            probs_hi(0, 0)
            turned_hi(t2_turned, t2_hi, 0, 0)
            tanh_scores(0, 0)
            combine_rows(0, 0)
            for e in range(NE):
                split_w(e)
            tanh_gate(0, 0, 0)
            tanh_gate(0, 0, 1)
            hidden_hi(0, 0, 0)
            with act.Fori(0, B - 1) as b:
                chunk(b, 0, True, False)
                chunk(b, 1, True, False)
            chunk(B - 1, 0, True, False)
            chunk(B - 1, 1, False, True)

        @block.vector
        def _(dve):
            V_ = nc.vector

            def setup():
                dve.wait_ge(small_loaded, 64)
                for i in range(2):
                    ins = V_.tensor_copy(bq2[:, :, i], bq_col[:])
                ins.then_inc(consts_set, 1)
                V_.memset(ptail[:].bitcast(U32), 0)
                V_.memset(Vtail[:].bitcast(U32), 0).then_inc(pads_set, 1)
                for m in range(KD):
                    dve.wait_ge(wq_turned, m + 1)
                    V_.tensor_copy(wqT[:, m, :], f_ps[m][:, 0:D]).then_inc(wqT_read, 1)
                for k in range(KD):
                    for n in range(2):
                        dve.wait_ge(a_hi, 2 * k + n + 1)
                        V_.scalar_tensor_tensor(
                            out=A[:, 2 * n:2 * n + 2, LO, k, :],
                            in0=(up_ps if k == 0 else f_ps)[n][:, 0:HALF].rearrange("p (b q) -> p b q", b=2),
                            scalar=SCALE, in1=A[:, 2 * n:2 * n + 2, HI, k, :].bitcast(F32),
                            op0=ALU.mult, op1=ALU.subtract).then_inc(a_lo, 1)
                dve.wait_ge(brow_scaled, 3)
                V_.scalar_tensor_tensor(out=Brow[:], in0=brow_hi[:].bitcast(F32), scalar=lo_row[:, 0:1],
                                        in1=brow_f[:], op0=ALU.mult, op1=ALU.add).then_inc(brow_split, 1)
                for bb in range(B):
                    dve.wait_ge(v_hi, 3 * bb + 3)
                    ps = gate_ps if bb % 2 == 0 else up_ps
                    V_.tensor_tensor(V[:, bb, LO, :], ps[0][:, 0:D], V[:, bb, HI, :].bitcast(F32), ALU.subtract) \
                        .then_inc(v_lo, 1)
                    V_.tensor_tensor(Vtail[64:64 + TAIL, bb, :], ps[1][0:TAIL, 0:D],
                                     Vtail[0:TAIL, bb, :].bitcast(F32), ALU.subtract).then_inc(v_lo, 1)
                dve.wait_ge(gate_inv, 1)
                V_.tensor_scalar(gw_n[:], gw_in[:], gsq[:, 2:3], None, ALU.mult).then_inc(gate_scaled, 1)
                dve.wait_ge(gate_split, 1)
                V_.tensor_tensor(G[:, :, E:2 * E], y_ps[0][:, 0:KD * E].rearrange("p (k e) -> p k e", k=KD),
                                 G[:, :, 0:E].bitcast(F32), ALU.subtract).then_inc(gate_split, 1)
                dve.wait_ge(mask_loaded, 16)
                dve.wait_ge(consts_set, 2)
                V_.memset(zero_keys, 0.0).then_inc(keep_set, 1)
                V_.memset(keep[:], MASKED).then_inc(keep_set, 1)
                dve.wait_ge(keep_set, 2)
                for t in range(S // P):
                    ins = V_.copy_predicated(keep[:, t, :], mask_in[:, t, :], zero_keys)
                ins.then_inc(keep_set, 1)
                dve.wait_ge(keep_set, 3)

            def split_w(e):
                dve.wait_ge(w_hi, e + 1)
                V_.tensor_tensor(W[:, e, LO, :], stage[:, e % STAGES, :], W[:, e, HI, :].bitcast(F32),
                                 ALU.subtract).then_inc(w_lo, 1)

            def ln_stats(src, done, b, hf, first):
                for j in range(TILES):
                    ins = V_.bn_stats(stats[:, j, :], src[:, j, :])
                ins.then_inc(bn_step, 1)
                wait_apart(dve, (bn_step, upto(b, hf, 2, 1 if first else 2)))
                for j in range(TILES):
                    ins = V_.bn_aggr(meanvar[:, j, :], stats[:, j, :])
                ins.then_inc(done, 1)

            def ln_scale(src, rstd_ready, done, b, hf):
                dve.wait_ge(rstd_ready, upto(b, hf, 1, 1))
                for j in range(TILES):
                    ins = V_.tensor_scalar(xn[:, j, :], src[:, j, :], meanvar[:, j, 0:1], rstd[:, j:j + 1],
                                           ALU.subtract, ALU.mult)
                ins.then_inc(done, 1)

            def ln1_stats_(b, hf):
                dve.wait_ge(x_loaded, upto(b, hf, 16, 16))
                ln_stats(xin, ln1_stats, b, hf, True)

            def ln1_scale_(b, hf):
                if not first_chunk(b, hf):
                    dve.wait_ge(t2_turned, upto(b, hf, 2, 0))
                ln_scale(xin, ln1_rstd, ln1_done, b, hf)

            def turned_lo(hi_done, done, b, hf):
                for k in range(KD):
                    dve.wait_ge(hi_done, upto(b, hf, 2, k + 1))
                    V_.tensor_tensor(xT[:, hf % 2, LO, k, :], f_ps[k][:], xT[:, hf % 2, HI, k, :].bitcast(F32),
                                     ALU.subtract).then_inc(done, 1)

            def mask_and_max(b, hf):
                for q in range(2):
                    wait_apart(dve, (scored, upto(b, hf, 2, q + 1)))
                    for j in (2 * q, 2 * q + 1):
                        ins = V_.tensor_tensor_reduce(att[:, j, :], f_ps[q][:, (j % 2) * D:(j % 2) * D + KEYS],
                                                      keep[:, (hf % 2) * TILES + j, :], 1.0, MASKED, ALU.add,
                                                      ALU.max, rsum[:, j:j + 1])
                    ins.then_inc(maxes, 1)
                    dve.wait_ge(maxes, upto(b, hf, 2, q + 1))
                    V_.tensor_scalar(nmax[:, 2 * q:2 * q + 2], rsum[:, 2 * q:2 * q + 2], -1.0, None, ALU.mult) \
                        .then_inc(maxed, 1)

            def sum_reciprocal(b, hf):
                dve.wait_ge(exped, upto(b, hf, TILES, TILES))
                dve.wait_ge(maxed, upto(b, hf, 2, 2))
                V_.reciprocal(rsum, esum).then_inc(rsummed, 1)

            def probs_lo(b, hf):
                dve.wait_ge(p_hi, upto(b, hf, 3, 1))
                V_.tensor_tensor(xT[:, hf % 2, LO, 0, :], f_ps[0][:], xT[:, hf % 2, HI, 0, :].bitcast(F32),
                                 ALU.subtract).then_inc(p_lo, 1)
                dve.wait_ge(p_hi, upto(b, hf, 3, 3))
                V_.tensor_tensor(ptail[32:32 + TAIL, :], f_ps[1][0:TAIL, :], ptail[0:TAIL, :].bitcast(F32),
                                 ALU.subtract).then_inc(p_lo, 1)

            def residual(b, hf):
                dve.wait_ge(rsummed, upto(b, hf, 1, 1))
                dve.wait_ge(stored, upto(b, hf, 16, 16))
                for q in range(2):
                    dve.wait_ge(attended, upto(b, hf, 2, q + 1))
                    for j in (2 * q, 2 * q + 1):
                        ins = V_.scalar_tensor_tensor(out=x2[:, hf % 2, j, :],
                                                      in0=f_ps[q][:, (j % 2) * D:(j % 2 + 1) * D],
                                                      scalar=rsum[:, j:j + 1], in1=xin[:, j, :],
                                                      op0=ALU.mult, op1=ALU.add)
                    ins.then_inc(x2_made, 1)

            def ln2_stats_(b, hf):
                dve.wait_ge(x2_made, upto(b, hf, 2, 2))
                ln_stats(x2[:, hf % 2], ln2_stats, b, hf, False)

            def ln2_scale_(b, hf):
                ln_scale(x2[:, hf % 2], ln2_rstd, ln2_done, b, hf)

            def sum_logits(b, hf):
                dve.wait_ge(routed_z, upto(b, hf, 1, 1))
                V_.tensor_reduce(z, f_ps[0][:, 0:TILES * 2 * E].rearrange("p (j t e) -> p j e t", j=TILES, t=2),
                                 AX_X, ALU.add).then_inc(z_summed, 1)

            def top_experts(b, hf):
                dve.wait_ge(tanh_z, upto(b, hf, 1, 1))
                V_.tensor_scalar(score, z, 0.5, 0.5, ALU.mult, ALU.add).then_inc(scores_set, 1)
                wait_apart(dve, (scores_set, upto(b, hf, 1, 1)))
                for j in range(TILES):
                    ins = V_.max(top8[:, j, :], score[:, j, :])
                ins.then_inc(topped, 1)
                wait_apart(dve, (topped, upto(b, hf, 1, 1)))
                for j in range(TILES):
                    V_.match_replace(rest[:, j, :], top8[:, j, :], score[:, j, :], 0.0).then_inc(rest_set, 1)
                V_.tensor_reduce(ssum, top8[:], AX_X, ALU.add).then_inc(rest_set, 1)
                dve.wait_ge(rest_set, upto(b, hf, TILES + 1, TILES + 1))
                V_.tensor_tensor(cw, score, rest, ALU.subtract).then_inc(picked, 1)
                V_.reciprocal(srec, ssum).then_inc(picked, 1)
                dve.wait_ge(picked, upto(b, hf, 2, 2))
                for j in range(TILES):
                    ins = V_.tensor_scalar(cw[:, j, :], cw[:, j, :], srec[:, j:j + 1], 0.5, ALU.mult, ALU.mult)
                ins.then_inc(combined, 1)

            def silu_up(b, hf, e):
                hf, e = nxt(hf, e)
                i = slot(hf, e)
                dve.wait_ge(tanh_done, upto(b, hf, NE, e + 1))
                V_.scalar_tensor_tensor(out=ew[:, i, :], in0=ew[:, i, :], scalar=1.0, in1=gate_ps[i][:],
                                        op0=ALU.add, op1=ALU.mult).then_inc(silu_done, 1)
                dve.wait_ge(silu_done, upto(b, hf, NE, e + 1 + FREE))
                dve.wait_ge(up_done, upto(b, hf, NE, e + 1))
                V_.tensor_tensor(ew[:, i, :], ew[:, i, :], up_ps[i][:], ALU.mult).then_inc(prod_done, 1)

            def hidden_lo(b, hf, e):
                hf, e = nxt(hf, e)
                i = slot(hf, e)
                dve.wait_ge(h_hi, upto(b, hf, NE, e + 1 + FREE))
                V_.tensor_tensor(hs[:, i, LO, :], h[:, i, :], hs[:, i, HI, :].bitcast(F32), ALU.subtract) \
                    .then_inc(h_lo, 1)

            def add_y(b, hf):
                for q in range(2):
                    dve.wait_ge(y_turned, upto(b, hf, 2, q + 1 + FREE))
                    v = x2[:, hf, 2 * q:2 * q + 2, :].rearrange("p j d -> p (j d)")
                    V_.tensor_tensor(v, v, f_ps[q][:], ALU.add).then_inc(y_added, 1)

            def chunk(b, hf, front, last):
                for s in range(NE):
                    if s + 2 < NE or not last:
                        silu_up(b, hf, s + 2)
                    if s + 1 < NE or not last:
                        hidden_lo(b, hf, s + 1)
                    if front:
                        if s == 0:
                            ln1_stats_(b, hf + 1)
                        if s == 1:
                            ln1_scale_(b, hf + 1)
                        if s == 2:
                            turned_lo(t1_hi, t1_lo, b, hf + 1)
                        if s == 4:
                            mask_and_max(b, hf + 1)
                        if s == 5:
                            sum_reciprocal(b, hf + 1)
                        if s == 7:
                            probs_lo(b, hf + 1)
                        if s == 9:
                            residual(b, hf + 1)
                            ln2_stats_(b, hf + 1)
                        if s == 10:
                            ln2_scale_(b, hf + 1)
                        if s == 12:
                            turned_lo(t2_hi, t2_lo, b, hf + 1)
                        if s == 14:
                            sum_logits(b, hf + 1)
                        if s == 15:
                            top_experts(b, hf + 1)
                add_y(b, hf)

            maxes = sem("maxes")
            for s_ in (silu_done, prod_done, h_lo):
                dve.sem_inc(s_, FREE)
            dve.sem_inc(y_added, FREE)
            ln1_stats_(0, 0)
            ln1_scale_(0, 0)
            setup()
            turned_lo(t1_hi, t1_lo, 0, 0)
            mask_and_max(0, 0)
            sum_reciprocal(0, 0)
            probs_lo(0, 0)
            residual(0, 0)
            ln2_stats_(0, 0)
            ln2_scale_(0, 0)
            turned_lo(t2_hi, t2_lo, 0, 0)
            sum_logits(0, 0)
            top_experts(0, 0)
            for e in range(NE):
                split_w(e)
            silu_up(0, 0, 0)
            silu_up(0, 0, 1)
            hidden_lo(0, 0, 0)
            with dve.Fori(0, B - 1) as b:
                chunk(b, 0, True, False)
                chunk(b, 1, True, False)
            chunk(B - 1, 0, True, False)
            chunk(B - 1, 1, False, True)

        @block.gpsimd
        def _(pool):
            pg = nc.gpsimd
            steps = [0]

            def setup():
                pg.memset(ident[:], 0.0).then_inc(pool_step, 1)
                pg.memset(lo_row[:], -1.0).then_inc(pool_step, 1)
                pg.memset(minus_half[:], -0.5)
                pg.memset(ones1[:], 1.0).then_inc(pool_step, 1)
                pool.wait_ge(pool_step, 3)
                pg.tensor_copy(ones2[:], ones1[:])
                pg.memset(lo_row[0:1, :], 0.0)
                pg.affine_select(out=ident[:], in_=ident[:], compare_op=ALU.not_equal, fill=1.0, base=0,
                                 pattern=[[-1, P]], channel_multiplier=1).then_inc(consts_set, 1)

            def gate_norm():
                pool.wait_ge(gate_summed, 1)
                pg.tensor_scalar(gsq[:, 1:2], gsq[:, 0:1], 1.0, NORM_EPS ** 2, ALU.mult, ALU.max) \
                    .then_inc(pool_step, 1)
                pool.wait_ge(pool_step, 4)
                pg.tensor_tensor(gsq[:, 2:3], gsq[:, 1:2], minus_half[0:E, 0:1], ALU.pow).then_inc(gate_inv, 1)

            def inverse_std(stats_ready, done, b, hf, spreads):
                waits = [(stats_ready, upto(b, hf, 1, 1))]
                if spreads:
                    waits.append((c_spread, upto(b, hf - 1, E, spreads)))
                wait_apart(pool, *waits)
                pg.tensor_scalar(var_eps, meanvar[:, :, 1], LN_EPS, 1.0, ALU.add, ALU.mult).then_inc(std_step, 1)
                first = stats_ready is ln1_stats
                pool.wait_ge(std_step, upto(b, hf, 2, 1 if first else 2))
                pg.tensor_tensor(rstd, var_eps, minus_half[:], ALU.pow).then_inc(done, 1)

            def inverse_norm(b, hf, spreads):
                pool.wait_ge(ln2_rstd, upto(b, hf, 1, 1))
                if spreads:
                    pool.wait_ge(c_spread, upto(b, hf - 1, E, spreads))
                pg.tensor_tensor(rsq, rstd, rstd, ALU.mult).then_inc(norm_step, 1)
                pool.wait_ge(norm_step, upto(b, hf, 3, 1))
                pg.tensor_tensor(nsq, rsq, meanvar[:, :, 1], ALU.mult).then_inc(norm_step, 1)
                wait_apart(pool, (norm_step, upto(b, hf, 3, 2)))
                pg.tensor_scalar(nsq, nsq, 4.0 * D, 4.0 * NORM_EPS ** 2, ALU.mult, ALU.max).then_inc(norm_step, 1)
                pool.wait_ge(norm_step, upto(b, hf, 3, 3))
                pg.tensor_tensor(inorm, nsq, minus_half[:], ALU.pow).then_inc(inv_norms, 1)

            def spread(b, hf, e):
                hf, e = nxt(hf, e)
                if e == 0:
                    return
                wait_apart(pool, (h_done, upto(b, hf, NE, e + FREE)), (crow_loaded, upto(b, hf, 64, 64)))
                r = e - 1
                pg.partition_broadcast(cb[:, e % 2, :], crow[32 * (r // 4):32 * (r // 4) + 1, r % 4, :]) \
                    .then_inc(c_spread, 1)

            def weighted(b, hf, e):
                hf, e = nxt(hf, e)
                i = slot(hf, e)
                if e == 0:
                    wait_apart(pool, (prod_done, upto(b, hf, NE, 1 + FREE)), (h_hi, upto(b, hf, NE, FREE - 1)),
                               (h_lo, upto(b, hf, NE, FREE - 1)))
                    pg.tensor_scalar(h[:, i, :], ew[:, i, :], 0.5, 1.0, ALU.mult, ALU.mult).then_inc(h_done, 1)
                else:
                    pool.wait_ge(prod_done, upto(b, hf, NE, e + 1 + FREE))
                    pool.wait_ge(h_hi, upto(b, hf, NE, e - 1 + FREE))
                    pool.wait_ge(h_lo, upto(b, hf, NE, e - 1 + FREE))
                    pool.wait_ge(c_spread, upto(b, hf, E, e))
                    pg.tensor_tensor(h[:, i, :], ew[:, i, :], cb[:, e % 2, :], ALU.mult).then_inc(h_done, 1)

            def chunk(b, hf, front, last):
                for s in range(NE):
                    if s + 1 < NE or not last:
                        weighted(b, hf, s + 1)
                    if s + 2 < NE or not last:
                        spread(b, hf, s + 2)
                    if front:
                        if s == 0:
                            inverse_std(ln1_stats, ln1_rstd, b, hf + 1, 2)
                        if s == 9:
                            inverse_std(ln2_stats, ln2_rstd, b, hf + 1, 11)
                        if s == 10:
                            inverse_norm(b, hf + 1, 12)

            std_step, norm_step = sem("std_step"), sem("norm_step")
            pool.sem_inc(h_done, FREE)
            setup()
            inverse_std(ln1_stats, ln1_rstd, 0, 0, 0)
            gate_norm()
            inverse_std(ln2_stats, ln2_rstd, 0, 0, 0)
            inverse_norm(0, 0, 0)
            weighted(0, 0, 0)
            spread(0, 0, 1)
            with pool.Fori(0, B - 1) as b:
                chunk(b, 0, True, False)
                chunk(b, 1, True, False)
            chunk(B - 1, 0, True, False)
            chunk(B - 1, 1, False, True)


_INS = ['x', 'ctx_1024', 'mask_SxS2_bk0', 'L0_xattn_Wq', 'L0_xattn_bq', 'L0_xattn_Wk', 'L0_xattn_bk',
        'L0_xattn_Wv', 'L0_xattn_bv', 'L0_ffn_gate_w', 'L0_ffn_w_gate', 'L0_ffn_w_up', 'L0_ffn_w_down',
        'L0_ffn_sw_gate', 'L0_ffn_sw_up', 'L0_ffn_sw_down']


def kernel(**inputs):
    import numpy as _np
    import concourse.bacc as _bacc
    from concourse.bass_utils import run_bass_kernel_spmd as _run

    nc = _bacc.Bacc("TRN2", target_bir_lowering=False, num_devices=1, dynamic_dma_scratch_size=1024)
    arrays, args = {}, []
    for name in _INS:
        a = _np.ascontiguousarray(inputs[name])
        arrays[f"in_{name}_dram"] = a
        args.append(nc.dram_tensor(f"in_{name}_dram", a.shape, mybir.dt.from_np(a.dtype), kind="ExternalInput").ap())
    out = nc.dram_tensor("out_0_dram", arrays["in_x_dram"].shape, F32, kind="ExternalOutput").ap()
    xattn_moe_kernel(nc, *args, out)
    r = _run(nc, [arrays], core_ids=[0])
    return r.results[0]["out_0_dram"]
```

```python
from contextlib import ExitStack

import concourse.bass as bass
from concourse import mybir

ALU = mybir.AluOpType
ACT = mybir.ActivationFunctionType
AX_X = mybir.AxisListType.X
F32 = mybir.dt.float32
F32R = mybir.dt.float32r
U32 = mybir.dt.uint32
U8 = mybir.dt.uint8

P = 128
LN_EPS = 1e-5
NORM_EPS = 1e-12
MASKED = -3e38
HI, LO = 0, 1

PE_AT = dict(turn_x=(2.5, 2.5), scores=(4.5, 5.5), turn_p=(7.5, 7.5), attend=(8.5, 8.5), turn_ln2=(11.5, 11.5),
             logits=(12.5,), turn_z=(13,), turn_c=(15,))
ACT_AT = dict(t1_hi=(3.5, 3.5), exps=(5.5, 6.5), probs_hi=(8.5, 8.5), t2_hi=(11.5, 11.5), read_z=(13,),
              tanh_scores=(13.5,), combine_rows=(15.5,))
DVE_AT = dict(ln1_stats=(1.5,), ln1_aggr=(1.5,), ln1_scale=(2.5, 2.5), t1_lo=(3.5, 3.5), maxes=(5.5, 6.5),
              sum_reciprocal=(7,), probs_lo=(8.5, 8.5), residual=(9.5, 9.5), ln2_stats=(9.5,), ln2_aggr=(9.5,),
              ln2_scale=(10.5, 10.5), t2_lo=(11.5, 11.5), sum_logits=(13.5,), top_eight=(14.5,),
              weights=(14.5,))
POOL_AT = dict(add_bias=(1.5,), ln1_std=(2.5,), ln2_std=(9.5,), inverse_norm=(10.5,))
SPLITS = dict(A0=range(0, 3), A1=range(3, 4), exps=range(4, 5), probs=range(5, 5), V3=range(5, 6),
              t2_hi=range(6, 8), tanh_scores=range(8, 10), tanh1=range(10, 13), hidden=range(13, 15),
              end=range(15, 17))
WARM = dict(start=16, attend=14, turn_ln2=30, logits=17, turn_z=6)


def xattn_moe_kernel(nc, x, ctx, mask, Wq, bq, Wk, bk, Wv, bv, gate_w, w_gate, w_up, w_down,
                     sw_gate, sw_up, sw_down, out):
    B, S, D = x.shape
    KEYS = ctx.shape[1]
    E, _, H = w_gate.shape
    TOK = 512
    TILES = TOK // P
    CHUNKS = B * S // TOK
    KD = D // P
    NE = E + 1
    TAIL = KEYS - P
    STACK = 96
    CKEYS = B * KEYS
    CT = -(-CKEYS // P)
    HALF = CKEYS // 2
    PAIRS = E // 2
    PLACES = 4
    WCOLS = 2 * KD * H + D
    UP0, DN0 = KD * H, 2 * KD * H
    SCALE = float(D) ** -0.5
    assert S == 2 * TOK and KD == 2 and H == P and 0 < TAIL <= 32 and E % 4 == 0 and NE % 2 == 1
    assert HALF <= 512 and CT * D + 2 * KD * CKEYS + D <= PLACES * 2 * TOK

    x_rows = x.rearrange("b s d -> (b s) d").rearrange("(c j p) d -> c p j d", p=P, j=TILES)
    c_rows = nc.dram_tensor("c_rows", [E, TOK], F32, kind="Internal").ap()
    out_rows = out.rearrange("b s d -> (b s) d").rearrange("(c j p) d -> c p j d", p=P, j=TILES)
    ctx_rows = ctx.rearrange("b s d -> (b s) d")

    with ExitStack() as stack:
        def sb(name, shape, dt=F32):
            return stack.enter_context(nc.sbuf_tensor(name, shape, dt))

        def sem(name):
            return stack.enter_context(nc.semaphore(name))

        W = sb("W", [P, NE, 2, WCOLS], F32R)
        A = sb("A", [P, B, KD, 2, KEYS], F32R)
        brow = sb("brow", [P, CKEYS])
        V = sb("V", [P, B, 2, D], F32R)
        Vtail = sb("Vtail", [STACK, B, D], F32R)
        G = sb("G", [P, KD, 2 * E], F32R)
        keep = sb("keep", [P, S // P, KEYS])
        ident = sb("ident", [P, P])
        minus_half = sb("minus_half", [P, TILES])
        xin = sb("xin", [P, TILES, D])
        x2 = sb("x2", [P, 2, TILES, D])
        xn = sb("xn", [P, TILES, D])
        xT = sb("xT", [P, 2, 2, KD, TOK], F32R)
        keepb = sb("keepb", [P, TILES, KEYS])
        att = sb("att", [P, TILES, KEYS])
        ptail = sb("ptail", [STACK, TOK], F32R)
        stats = sb("stats", [P, TILES, 6])
        meanvar = sb("meanvar", [P, TILES, 2])
        small = sb("small", [P, 10, TILES])
        var_eps, rstd, nmax, esum, rsum, rsq, nsq, inorm, ssum, srec = (small[:, i, :] for i in range(10))
        route = sb("route", [P, 4, TILES, E])
        z, score, rest, cw = (route[:, i] for i in range(4))
        top8 = sb("top8", [P, TILES, 8])
        cT = sb("cT", [P, TOK])
        cb = sb("cb", [P, PLACES, 2, TOK])
        hidden = sb("hidden", [P, 2, 2, TOK])
        ew = hidden[:, 0]
        h = hidden[:, 1]
        hs = sb("hs", [P, 2, 2, TOK], F32R)
        zT = sb("zT", [2 * E, TOK])
        STAGES = 3
        stage = sb("stage", [P, STAGES, WCOLS])
        cb_flat = cb[:].rearrange("p a b t -> p (a b t)")
        KD_KEYS = KD * CKEYS
        ctx_in = cb_flat[:, 0:CT * D].rearrange("p (t d) -> p t d", t=CT)
        wk_in = x2[:, 1, 0:KD, :]
        wq_in = x2[:, 0, 0:KD, :]
        wv_in = x2[:, 1, KD:2 * KD, :]
        ctxT = cb_flat[:, CT * D:CT * D + KD_KEYS].rearrange("p (k c) -> p k c", k=KD)
        wqT = hidden[:, 0, 0:KD, 0:D]
        KT = cb_flat[:, CT * D + KD_KEYS:CT * D + 2 * KD_KEYS].rearrange("p (k c) -> p k c", k=KD)
        bk_col = sb("bk_col", [P, KD])
        bq_col = sb("bq_col", [P, KD])
        bq_rep = hidden[:, 1, 0, 0:KD * P].rearrange("p (k m) -> p k m", k=KD)
        bv_row = hidden[0:1, 1, 1, 0:D]
        ones1 = sb("ones1", [1, P])
        gw_in = cb_flat[0:E, CT * D + 2 * KD_KEYS:CT * D + 2 * KD_KEYS + D]
        gw_n = zT[0:E, 0:D]
        gsq = sb("gsq", [E, 4])
        mask_in = cT[:].bitcast(U8)[:, 0:S // P * KEYS].rearrange("p (t k) -> p t k", k=KEYS)
        zero_keys = att[:, 0, :]

        def bank(name):
            return stack.enter_context(nc.psum_tensor(name, [P, 512], F32))

        gate_ps = [bank(f"gate_ps{i}") for i in range(2)]
        up_ps = [bank(f"up_ps{i}") for i in range(2)]
        y_ps = [bank(f"y_ps{i}") for i in range(2)]
        f_ps = [bank(f"f_ps{i}") for i in range(2)]

        v_ps = [up_ps, up_ps, gate_ps, gate_ps]

        (ctx_loaded, wk_loaded, wq_loaded, wv_loaded, bk_loaded, bq_loaded, gw_loaded, mask_loaded, x_loaded,
         stored, c_stored) = (
            sem(n) for n in ("ctx_loaded", "wk_loaded", "wq_loaded", "wv_loaded", "bk_loaded", "bq_loaded",
                             "gw_loaded", "mask_loaded", "x_loaded", "stored", "c_stored"))
        cb_loaded = [sem(f"cb_loaded{i}") for i in range(PLACES)]
        staged = [sem(f"staged{i}") for i in range(STAGES)]
        (consts_set, ctx_turned, ctxT_read, wq_turned, wqT_read, kt_made, kt_read, a_made, a_hi, a_lo, brow_made,
         brow_scaled, v_made, v_hi, v_lo, gate_summed, gate_inv, gate_scaled, gate_turned, gate_split,
         keep_set, pads_set, w_hi, w_lo) = (
            sem(n) for n in ("consts_set", "ctx_turned", "ctxT_read", "wq_turned", "wqT_read", "kt_made", "kt_read",
                             "a_made", "a_hi", "a_lo", "brow_made", "brow_scaled", "v_made", "v_hi", "v_lo",
                             "gate_summed", "gate_inv", "gate_scaled", "gate_turned", "gate_split", "keep_set",
                             "pads_set", "w_hi", "w_lo"))
        (ln1_stats, ln1_rstd, ln1_done, t1_turned, t1_hi, t1_lo, bias_added, scored, lo_added, maxes, maxed,
         exped, rsummed, p_turned, p_hi, p_lo, attended, x2_made, ln2_stats, ln2_rstd, inv_norms, ln2_done,
         t2_turned, t2_hi, t2_lo, routed_z, z_read, z_turned, z_summed, tanh_z, scores_set, topped, rest_set,
         picked, combined, c_turned, c_read, bn_step, pool_step, std_step, norm_step) = (
            sem(n) for n in ("ln1_stats", "ln1_rstd", "ln1_done", "t1_turned", "t1_hi", "t1_lo", "bias_added",
                             "scored", "lo_added", "maxes", "maxed", "exped", "rsummed", "p_turned", "p_hi", "p_lo",
                             "attended", "x2_made", "ln2_stats", "ln2_rstd", "inv_norms", "ln2_done", "t2_turned",
                             "t2_hi", "t2_lo", "routed_z", "z_read", "z_turned", "z_summed", "tanh_z", "scores_set",
                             "topped", "rest_set", "picked", "combined", "c_turned", "c_read", "bn_step", "pool_step",
                             "std_step", "norm_step"))
        (gate_done, up_done, tanh_done, silu_done, prod_done, h_done, h_hi, h_lo, down_done, y_half, y_added) = (
            sem(n) for n in ("gate_done", "up_done", "tanh_done", "silu_done", "prod_done", "h_done",
                             "h_hi", "h_lo", "down_done", "y_half", "y_added"))

        FREE = 2

        def upto(b, hf, per, k):
            return b * (2 * per) + (per * hf + k)

        def first_chunk(b, hf):
            return isinstance(b, int) and b == 0 and hf == 0

        def wait_apart(eng, *waits):
            counts = [n if isinstance(n, int) else eng.to_reg(n) for _, n in waits]
            eng.wait_ge(consts_set, 1)
            for (what, _), n in zip(waits, counts):
                eng.wait_ge(what, n)

        def due(table, step, at):
            return [part for part, place in enumerate(table[step]) if place == at]

        def slot(hf, e):
            return (NE * hf + e) % 2

        def nxt(hf, e):
            return (hf, e) if e < NE else (hf + 1, e - NE)

        block = stack.enter_context(nc.Block())

        @block.sync
        def _(sp):
            sp.sem_inc(stored, 16 * FREE)
            sp.dma_start(ctx_in[:, 0:CT - 1, :], ctx_rows[0:(CT - 1) * P, :].rearrange("(t p) d -> p t d", p=P)) \
                .then_inc(ctx_loaded, 16)
            sp.dma_start(ctx_in[0:CKEYS - (CT - 1) * P, CT - 1, :], ctx_rows[(CT - 1) * P:CKEYS, :]) \
                .then_inc(ctx_loaded, 16)
            sp.dma_start(wk_in[:], Wk.rearrange("(k p) e -> p k e", p=P)).then_inc(wk_loaded, 16)
            sp.dma_start(wq_in, Wq.rearrange("(k p) e -> p k e", p=P)).then_inc(wq_loaded, 16)
            sp.dma_start(bk_col[:], bk.rearrange("(k p) -> p k", p=P), allow_slow_non_contiguous=True) \
                .then_inc(bk_loaded, 16)
            sp.dma_start(xin[:], x_rows[0]).then_inc(x_loaded, 16)
            sp.dma_start(wv_in, Wv.rearrange("(k p) e -> p k e", p=P)).then_inc(wv_loaded, 16)
            sp.dma_start(bv_row, bv.rearrange("(a d) -> a d", a=1)).then_inc(wv_loaded, 16)
            sp.dma_start(bq_col[:], bq.rearrange("(k p) -> p k", p=P), allow_slow_non_contiguous=True) \
                .then_inc(bq_loaded, 16)
            sp.dma_start(mask_in[:], mask.rearrange("(t p) k -> p t k", p=P)).then_inc(mask_loaded, 16)
            sp.dma_start(gw_in, gate_w).then_inc(gw_loaded, 16)
            for e in range(NE):
                if e >= STAGES:
                    sp.wait_ge(w_hi, e - STAGES + 1)
                    sp.wait_ge(w_lo, e - STAGES + 1)
                g, u, d = (sw_gate, sw_up, sw_down) if e == 0 else (w_gate[e - 1], w_up[e - 1], w_down[e - 1])
                s = stage[:, e % STAGES, :]
                sp.dma_start(s[:, 0:UP0].rearrange("p (k h) -> p k h", k=KD), g.rearrange("(k p) h -> p k h", p=P)) \
                    .then_inc(staged[e % STAGES], 16)
                sp.dma_start(s[:, UP0:DN0].rearrange("p (k h) -> p k h", k=KD), u.rearrange("(k p) h -> p k h", p=P)) \
                    .then_inc(staged[e % STAGES], 16)
                sp.dma_start(s[:, DN0:WCOLS], d).then_inc(staged[e % STAGES], 16)
            sp.wait_ge(x2_made, 2)
            sp.dma_start(xin[:], x_rows[1]).then_inc(x_loaded, 16)

            def spread(b, hf, pair):
                stored_c = (c_stored, upto(b, hf, 16, 16))
                if pair >= PLACES:
                    wait_apart(sp, (h_done, upto(b, hf, NE, 2 * (pair - PLACES) + 3 + FREE)))
                elif first_chunk(b, hf):
                    wait_apart(sp, stored_c)
                else:
                    wait_apart(sp, (h_done, upto(b, hf - 1, NE, 2 * (pair + PLACES) + 3 + FREE)), stored_c)
                sp.dma_start(cb[:, pair % PLACES].rearrange("p a t -> p (a t)"),
                             c_rows[2 * pair:2 * pair + 2, :].rearrange("a t -> (a t)").partition_broadcast(P)) \
                    .then_inc(cb_loaded[pair % PLACES], 16)

            for pair in range(PLACES):
                spread(0, 0, pair)

            def chunk(b, hf, load):
                for pair in range(PLACES, PAIRS):
                    spread(b, hf, pair)
                if load:
                    sp.wait_ge(x2_made, upto(b, hf, 2, 4))
                    sp.dma_start(xin[:], x_rows[b * 2 + (hf + 2)]).then_inc(x_loaded, 16)
                for pair in range(PLACES):
                    spread(b, hf + 1, pair)
                sp.wait_ge(y_added, upto(b, hf, 2, 2 + FREE))
                sp.dma_start(out_rows[b * 2 + hf], x2[:, hf]).then_inc(stored, 16)

            def last_stores():
                for q in range(2):
                    sp.wait_ge(y_added, 2 * CHUNKS + FREE - 1 + q)
                    sp.dma_start(out_rows[CHUNKS - 1, :, 2 * q:2 * q + 2, :], x2[:, 1, 2 * q:2 * q + 2, :]) \
                        .then_inc(stored, 16)

            with sp.Fori(0, B - 1) as b:
                chunk(b, 0, True)
                chunk(b, 1, True)
            chunk(B - 1, 0, False)
            for pair in range(PLACES, PAIRS):
                spread(B - 1, 1, pair)
            last_stores()
            sp.wait_ge(stored, 16 * (CHUNKS + 1 + FREE))

        @block.tensor
        def _(pe):
            mm = nc.tensor.matmul

            def three_pass(ps, pairs, first, last):
                for i, ((lh, ll), (rh, rl)) in enumerate(pairs):
                    mm(ps, lh, rh, start=first and i == 0, stop=False)
                    mm(ps, lh, rl, start=False, stop=False)
                    ins = mm(ps, ll, rh, start=False, stop=last and i == len(pairs) - 1)
                return ins

            def keep_warm(step):
                for _ in range(WARM[step]):
                    nc.tensor.transpose(up_ps[0][:, 0:P], ident[:], ident[:])

            def turn_inputs():
                pe.wait_ge(consts_set, 1)
                keep_warm("start")
                pe.wait_ge(ctx_loaded, 32)
                for k in range(KD):
                    for t in range(CT):
                        n = min(P, CKEYS - t * P)
                        to = gate_ps[k][:, t * P:t * P + n] if t < 4 else up_ps[k][:, 0:n]
                        ins = nc.tensor.transpose(to, ctx_in[0:n, t, k * P:(k + 1) * P], ident[0:n, 0:n])
                    ins.then_inc(ctx_turned, 1)
                pe.wait_ge(wq_loaded, 16)
                for m in range(KD):
                    for k in range(KD):
                        ins = nc.tensor.transpose(f_ps[m][:, k * P:(k + 1) * P], wq_in[:, k, m * P:(m + 1) * P],
                                                  ident[:])
                    ins.then_inc(wq_turned, 1)

            def project():
                pe.wait_ge(wk_loaded, 16)
                pe.wait_ge(ctxT_read, 4)
                for m in range(KD):
                    for n in range(2):
                        to = (y_ps if m == 0 else gate_ps)[n][:, 0:HALF]
                        for k in range(KD):
                            ins = mm(to, wk_in[:, k, m * P:(m + 1) * P], ctxT[:, k, n * HALF:(n + 1) * HALF],
                                     start=k == 0, stop=k == KD - 1)
                        ins.then_inc(kt_made, 1)
                pe.wait_ge(wqT_read, 2)
                turn_x(0, 0, 0)
                turn_x(0, 0, 1)
                pe.wait_ge(kt_read, 4)
                for k in range(KD):
                    for n in range(2):
                        to = (y_ps if k == 0 else gate_ps)[n][:, 0:HALF]
                        for m in range(KD):
                            ins = mm(to, wqT[:, m, k * P:(k + 1) * P], KT[:, m, n * HALF:(n + 1) * HALF],
                                     start=m == 0, stop=m == KD - 1)
                        ins.then_inc(a_made, 1)
                    if k == 0:
                        pe.wait_ge(consts_set, 2)
                        pe.wait_ge(t1_lo, 2)
                        for n in range(2):
                            for m in range(KD):
                                ins = mm(f_ps[n][:, 0:HALF], bq_rep[:, m, :], KT[:, m, n * HALF:(n + 1) * HALF],
                                         start=m == 0, stop=m == KD - 1)
                            ins.then_inc(brow_made, 1)

            def values(bb):
                if bb == 0:
                    pe.wait_ge(wv_loaded, 32)
                if bb % 2:
                    pe.wait_ge(v_hi, 3 * bb)
                    pe.wait_ge(v_lo, 2 * bb)
                for t, (r0, n) in enumerate(((0, P), (P, TAIL))):
                    to = v_ps[bb][t][0:n, 0:D]
                    for k in range(KD):
                        mm(to, ctxT[:, k, bb * KEYS + r0:bb * KEYS + r0 + n], wv_in[:, k, :], start=k == 0,
                           stop=False)
                    ins = mm(to, ones1[0:1, 0:n], bv_row[0:1, :], start=False, stop=True)
                ins.then_inc(v_made, 1)

            def turn_router():
                pe.wait_ge(gate_scaled, 1)
                pe.wait_ge(a_lo, 2)
                for k in range(KD):
                    ins = nc.tensor.transpose(y_ps[0][:, k * E:(k + 1) * E], gw_n[:, k * P:(k + 1) * P],
                                              ident[0:E, 0:E])
                ins.then_inc(gate_turned, 1)

            def turn_ln(ready, turned, b, hf, k):
                if k == 0:
                    pe.wait_ge(ready, upto(b, hf, 2, 2))
                for j in range(TILES):
                    ins = nc.tensor.transpose(f_ps[k][:, j * P:(j + 1) * P], xn[:, j, k * P:(k + 1) * P], ident[:])
                ins.then_inc(turned, 1)

            def turn_x(b, hf, k):
                if k == 0 and not first_chunk(b, hf):
                    pe.wait_ge(c_read, upto(b, hf, 1, 0))
                turn_ln(ln1_done, t1_turned, b, hf, k)

            def turn_ln2(b, hf, k):
                turn_ln(ln2_done, t2_turned, b, hf, k)

            def scores(b, hf, q):
                if q == 0:
                    pe.wait_ge(t1_hi, upto(b, hf, 2, 2))
                    pe.wait_ge(t1_lo, upto(b, hf, 2, 2))
                else:
                    pe.wait_ge(maxes, upto(b, hf, 2, 1))
                par, bi = hf % 2, b + hf // 2
                for j in (2 * q, 2 * q + 1):
                    to, c = f_ps[j % 2], slice(j * P, (j + 1) * P)
                    for k in range(KD):
                        mm(to[:, 0:2 * KEYS], xT[:, par, HI, k, c], A[:, bi, k].rearrange("p s q -> p (s q)"),
                           start=k == 0, stop=False)
                        ins = mm(to[:, 0:KEYS], xT[:, par, LO, k, c], A[:, bi, k, HI, :], start=False,
                                 stop=k == KD - 1)
                ins.then_inc(scored, 1)

            def turn_p(b, hf, q):
                if q == 0:
                    pe.wait_ge(exped, upto(b, hf, TILES, TILES))
                c0, n = ((0, P), (P, TAIL))[q]
                for j in range(TILES):
                    ins = nc.tensor.transpose(f_ps[q][0:n, j * P:(j + 1) * P], att[:, j, c0:c0 + n], ident[:])
                ins.then_inc(p_turned, 1)

            def attend(b, hf, q):
                if q == 0:
                    pe.wait_ge(p_hi, upto(b, hf, 3, 3))
                    pe.wait_ge(p_lo, upto(b, hf, 2, 2))
                par, bi = hf % 2, b + hf // 2
                for j in (2 * q, 2 * q + 1):
                    to = f_ps[q][:, (j % 2) * D:(j % 2 + 1) * D]
                    c = slice(j * P, (j + 1) * P)
                    three_pass(to, [((xT[:, par, HI, 0, c], xT[:, par, LO, 0, c]), (V[:, bi, HI, :], V[:, bi, LO, :]))],
                               first=True, last=False)
                    ins = mm(to, ptail[:, c], Vtail[:, bi, :], start=False, stop=True)
                ins.then_inc(attended, 1)

            def logits(b, hf):
                pe.wait_ge(t2_hi, upto(b, hf, 2, 2))
                pe.wait_ge(t2_lo, upto(b, hf, 2, 2))
                par = hf % 2
                for k in range(KD):
                    mm(f_ps[0][0:2 * E, :], G[:, k, :], xT[:, par, HI, k, :], start=k == 0, stop=False)
                for k in range(KD):
                    ins = mm(f_ps[0][0:E, :], G[:, k, 0:E], xT[:, par, LO, k, :], start=False, stop=k == KD - 1)
                ins.then_inc(routed_z, 1)

            def turn_z(b, hf):
                wait_apart(pe, (z_read, upto(b, hf, 1, 1)))
                for j in range(TILES):
                    ins = nc.tensor.transpose(f_ps[0][:, j * 2 * E:(j + 1) * 2 * E], zT[:, j * P:(j + 1) * P],
                                              ident[0:2 * E, 0:2 * E])
                ins.then_inc(z_turned, 1)

            def turn_c(b, hf):
                pe.wait_ge(combined, upto(b, hf, 1, 1))
                for j in range(TILES):
                    ins = nc.tensor.transpose(f_ps[1][0:E, j * P:(j + 1) * P], cw[:, j, :], ident[:])
                ins.then_inc(c_turned, 1)

            def gate_up(b, hf, e):
                hf, e = nxt(hf, e)
                i, par = slot(hf, e), hf % 2
                if e == 0:
                    pe.wait_ge(t2_hi, upto(b, hf, 2, 2))
                    pe.wait_ge(t2_lo, upto(b, hf, 2, 2))
                if hf == 0:
                    pe.wait_ge(w_hi, e + 1)
                    pe.wait_ge(w_lo, e + 1)
                for ps, col, free, done in ((gate_ps, 0, silu_done, gate_done), (up_ps, UP0, prod_done, up_done)):
                    pe.wait_ge(free, upto(b, hf, NE, e - 1 + FREE))
                    ins = three_pass(ps[i][:], [((W[:, e, HI, col + k * H:col + (k + 1) * H],
                                                  W[:, e, LO, col + k * H:col + (k + 1) * H]),
                                                 (xT[:, par, HI, k, :], xT[:, par, LO, k, :])) for k in range(KD)],
                                     first=True, last=True)
                    ins.then_inc(done, 1)

            def down(b, hf, e):
                i = slot(hf, e)
                pe.wait_ge(h_hi, upto(b, hf, NE, e + 1 + FREE))
                pe.wait_ge(h_lo, upto(b, hf, NE, e + 1 + FREE))
                if e == 0:
                    pe.wait_ge(y_added, upto(b, hf, 2, FREE))
                for j in range(TILES):
                    c = slice(j * P, (j + 1) * P)
                    ins = three_pass(y_ps[j // 2][:, (j % 2) * D:(j % 2 + 1) * D],
                                     [((hs[:, i, HI, c], hs[:, i, LO, c]),
                                       (W[:, e, HI, DN0:DN0 + D], W[:, e, LO, DN0:DN0 + D]))],
                                     first=e == 0 and j % 2 == 0, last=e == NE - 1 and j % 2 == 1)
                    if e == NE - 1 and j == 1:
                        ins.then_inc(y_half, 1)
                ins.then_inc(down_done, 1)

            def front(at, b, hf):
                for part in due(PE_AT, "turn_x", at):
                    turn_x(b, hf, part)
                for part in due(PE_AT, "scores", at):
                    scores(b, hf, part)
                for part in due(PE_AT, "turn_p", at):
                    turn_p(b, hf, part)
                for part in due(PE_AT, "attend", at):
                    attend(b, hf, part)
                for part in due(PE_AT, "turn_ln2", at):
                    turn_ln2(b, hf, part)
                if due(PE_AT, "logits", at):
                    logits(b, hf)
                if due(PE_AT, "turn_z", at):
                    turn_z(b, hf)
                if due(PE_AT, "turn_c", at):
                    turn_c(b, hf)

            def chunk(b, hf, ahead, last):
                for s in range(NE):
                    down(b, hf, s)
                    if ahead:
                        front(s, b, hf + 1)
                    if s + 3 < NE or not last:
                        gate_up(b, hf, s + 3)
                    if ahead:
                        front(s + .5, b, hf + 1)

            pe.sem_inc(down_done, FREE)
            turn_inputs()
            project()
            values(0)
            pe.wait_ge(brow_scaled, 2)
            pe.wait_ge(a_lo, 4)
            scores(0, 0, 0)
            values(1)
            scores(0, 0, 1)
            values(2)
            turn_p(0, 0, 0)
            turn_p(0, 0, 1)
            keep_warm("attend")
            pe.wait_ge(v_lo, 2)
            attend(0, 0, 0)
            attend(0, 0, 1)
            values(3)
            turn_router()
            keep_warm("turn_ln2")
            turn_ln2(0, 0, 0)
            turn_ln2(0, 0, 1)
            keep_warm("logits")
            pe.wait_ge(gate_split, 2)
            logits(0, 0)
            keep_warm("turn_z")
            turn_z(0, 0)
            pe.wait_ge(v_hi, 3 * B)
            pe.wait_ge(v_lo, 2 * B)
            gate_up(0, 0, 0)
            turn_c(0, 0)
            gate_up(0, 0, 1)
            gate_up(0, 0, 2)
            with pe.Fori(0, B - 1) as b:
                chunk(b, 0, True, False)
                chunk(b, 1, True, False)
            chunk(B - 1, 0, True, False)
            chunk(B - 1, 1, False, True)

        @block.scalar
        def _(act):
            af = nc.scalar.activation

            def read_ctx():
                act.wait_ge(ctx_turned, 1)
                af(ctxT[:, 0, 0:4 * P], gate_ps[0][:], ACT.Copy).then_inc(ctxT_read, 1)
                af(ctxT[:, 0, 4 * P:CKEYS], up_ps[0][:, 0:CKEYS - 4 * P], ACT.Copy).then_inc(ctxT_read, 1)

            def read_keys():
                act.wait_ge(bk_loaded, 16)
                for m in range(KD):
                    for n in range(2):
                        act.wait_ge(kt_made, 2 * m + n + 1)
                        af(KT[:, m, n * HALF:(n + 1) * HALF], (y_ps if m == 0 else gate_ps)[n][:, 0:HALF],
                           ACT.Identity, bias=bk_col[:, m:m + 1]).then_inc(kt_read, 1)

            def write_a_hi(k):
                for n in range(2):
                    act.wait_ge(a_made, 2 * k + n + 1)
                    af(A[:, 2 * n:2 * n + 2, k, HI, :],
                       (y_ps if k == 0 else gate_ps)[n][:, 0:HALF].rearrange("p (b q) -> p b q", b=2),
                       ACT.Copy, scale=SCALE).then_inc(a_hi, 1)

            def bias_row():
                for n in range(2):
                    act.wait_ge(brow_made, n + 1)
                    af(brow[:, n * HALF:(n + 1) * HALF], f_ps[n][:, 0:HALF], ACT.Copy, scale=SCALE) \
                        .then_inc(brow_scaled, 1)

            def write_v_hi(bb):
                act.wait_ge(v_made, bb + 1)
                ps = v_ps[bb]
                af(V[:, bb, HI, :], ps[0][:, 0:D], ACT.Copy).then_inc(v_hi, 1)
                af(Vtail[0:TAIL, bb, :], ps[1][0:TAIL, 0:D], ACT.Copy).then_inc(v_hi, 1)
                af(Vtail[32:32 + TAIL, bb, :], ps[1][0:TAIL, 0:D], ACT.Copy).then_inc(v_hi, 1)

            def router_norms():
                act.wait_ge(gw_loaded, 16)
                af(gw_n, gw_in, ACT.Square, accum_out=gsq[:, 0:1]).then_inc(gate_summed, 1)

            def router_hi():
                act.wait_ge(gate_turned, 1)
                af(G[:, :, 0:E], y_ps[0][:, 0:KD * E].rearrange("p (k e) -> p k e", k=KD), ACT.Copy) \
                    .then_inc(gate_split, 1)

            def split_w(e):
                act.wait_ge(staged[e % STAGES], 48 * (e // STAGES + 1))
                af(W[:, e, HI, :], stage[:, e % STAGES, :], ACT.Copy).then_inc(w_hi, 1)

            def turned_hi(turned, done, b, hf, k):
                act.wait_ge(turned, upto(b, hf, 2, k + 1))
                af(xT[:, hf % 2, HI, k, :], f_ps[k][:], ACT.Copy).then_inc(done, 1)

            def write_t1_hi(b, hf, k):
                turned_hi(t1_turned, t1_hi, b, hf, k)

            def write_t2_hi(b, hf, k):
                turned_hi(t2_turned, t2_hi, b, hf, k)

            def exps(b, hf, q):
                act.wait_ge(maxed, upto(b, hf, 2, q + 1))
                for j in (2 * q, 2 * q + 1):
                    af(att[:, j, :], att[:, j, :], ACT.Exp, bias=nmax[:, j:j + 1], accum_out=esum[:, j:j + 1]) \
                        .then_inc(exped, 1)

            def write_probs_hi(b, hf, q):
                act.wait_ge(p_turned, upto(b, hf, 2, q + 1))
                if q == 0:
                    af(xT[:, hf % 2, HI, 0, :], f_ps[0][:], ACT.Copy).then_inc(p_hi, 1)
                else:
                    af(ptail[0:TAIL, :], f_ps[1][0:TAIL, :], ACT.Copy).then_inc(p_hi, 1)
                    af(ptail[64:64 + TAIL, :], f_ps[1][0:TAIL, :], ACT.Copy).then_inc(p_hi, 1)

            def read_z(b, hf):
                act.wait_ge(routed_z, upto(b, hf, 1, 1))
                af(zT[:], f_ps[0][0:2 * E, :], ACT.Copy).then_inc(z_read, 1)

            def tanh_scores(b, hf):
                act.wait_ge(z_summed, upto(b, hf, 1, 1))
                act.wait_ge(inv_norms, upto(b, hf, 1, 1))
                for j in range(TILES):
                    ins = af(z[:, j, :], z[:, j, :], ACT.Tanh, scale=inorm[:, j:j + 1])
                ins.then_inc(tanh_z, 1)

            def combine_rows(b, hf):
                act.wait_ge(c_turned, upto(b, hf, 1, 1))
                if not first_chunk(b, hf):
                    act.wait_ge(c_stored, upto(b, hf, 16, 0))
                af(cT[0:E, :], f_ps[1][0:E, :], ACT.Copy).then_inc(c_read, 1)
                act.wait_ge(c_read, upto(b, hf, 1, 1))
                if not first_chunk(b, hf):
                    for done in cb_loaded:
                        act.wait_ge(done, upto(b, hf, 32, 0))
                act.dma_start(c_rows, cT[0:E, :]).then_inc(c_stored, 16)

            def tanh_gate(b, hf, e):
                hf, e = nxt(hf, e)
                i = slot(hf, e)
                act.wait_ge(gate_done, upto(b, hf, NE, e + 1))
                act.wait_ge(h_done, upto(b, hf, NE, e - 1 + FREE))
                af(ew[:, i, :], gate_ps[i][:], ACT.Tanh, scale=0.5).then_inc(tanh_done, 1)

            def hidden_hi(b, hf, e):
                hf, e = nxt(hf, e)
                i = slot(hf, e)
                act.wait_ge(h_done, upto(b, hf, NE, e + 1 + FREE))
                act.wait_ge(down_done, upto(b, hf, NE, e - 1 + FREE))
                af(hs[:, i, HI, :], h[:, i, :], ACT.Copy).then_inc(h_hi, 1)

            def front(at, b, hf):
                for part in due(ACT_AT, "t1_hi", at):
                    write_t1_hi(b, hf, part)
                for part in due(ACT_AT, "exps", at):
                    exps(b, hf, part)
                for part in due(ACT_AT, "probs_hi", at):
                    write_probs_hi(b, hf, part)
                for part in due(ACT_AT, "t2_hi", at):
                    write_t2_hi(b, hf, part)
                if due(ACT_AT, "read_z", at):
                    read_z(b, hf)
                if due(ACT_AT, "tanh_scores", at):
                    tanh_scores(b, hf)
                if due(ACT_AT, "combine_rows", at):
                    combine_rows(b, hf)

            def chunk(b, hf, ahead, last):
                for s in range(NE):
                    if s + 2 < NE or not last:
                        tanh_gate(b, hf, s + 2)
                    if ahead:
                        front(s, b, hf + 1)
                    if s + 1 < NE or not last:
                        hidden_hi(b, hf, s + 1)
                    if ahead:
                        front(s + .5, b, hf + 1)

            act.sem_inc(h_hi, FREE)
            read_ctx()
            read_keys()
            write_t1_hi(0, 0, 0)
            write_t1_hi(0, 0, 1)
            for e in SPLITS["A0"]:
                split_w(e)
            write_a_hi(0)
            bias_row()
            for e in SPLITS["A1"]:
                split_w(e)
            write_a_hi(1)
            act.wait_ge(pads_set, 2)
            write_v_hi(0)
            router_norms()
            for e in SPLITS["exps"]:
                split_w(e)
            exps(0, 0, 0)
            write_v_hi(1)
            exps(0, 0, 1)
            write_v_hi(2)
            for e in SPLITS["probs"]:
                split_w(e)
            write_probs_hi(0, 0, 0)
            write_probs_hi(0, 0, 1)
            for e in SPLITS["V3"]:
                split_w(e)
            write_v_hi(3)
            router_hi()
            for e in SPLITS["t2_hi"]:
                split_w(e)
            write_t2_hi(0, 0, 0)
            write_t2_hi(0, 0, 1)
            read_z(0, 0)
            for e in SPLITS["tanh_scores"]:
                split_w(e)
            tanh_scores(0, 0)
            tanh_gate(0, 0, 0)
            for e in SPLITS["tanh1"]:
                split_w(e)
            combine_rows(0, 0)
            tanh_gate(0, 0, 1)
            for e in SPLITS["hidden"]:
                split_w(e)
            hidden_hi(0, 0, 0)
            for e in SPLITS["end"]:
                split_w(e)
            with act.Fori(0, B - 1) as b:
                chunk(b, 0, True, False)
                chunk(b, 1, True, False)
            chunk(B - 1, 0, True, False)
            chunk(B - 1, 1, False, True)

        @block.vector
        def _(dve):
            V_ = nc.vector

            def pads():
                dve.wait_ge(bq_loaded, 16)
                dve.wait_ge(consts_set, 1)
                for m in range(KD):
                    ins = V_.tensor_scalar(bq_rep[:, m, :], ident[:], 0.0, bq_col[:, m:m + 1], ALU.mult, ALU.add)
                ins.then_inc(consts_set, 1)

            def write_wqT():
                for m in range(KD):
                    dve.wait_ge(wq_turned, m + 1)
                    V_.tensor_copy(wqT[:, m, :], f_ps[m][:, 0:D]).then_inc(wqT_read, 1)

            def read_ctx():
                dve.wait_ge(ctx_turned, 2)
                V_.tensor_copy(ctxT[:, 1, 0:4 * P], gate_ps[1][:]).then_inc(ctxT_read, 1)
                V_.tensor_copy(ctxT[:, 1, 4 * P:CKEYS], up_ps[1][:, 0:CKEYS - 4 * P]).then_inc(ctxT_read, 1)

            def write_a_lo(k):
                for n in range(2):
                    dve.wait_ge(a_hi, 2 * k + n + 1)
                    V_.scalar_tensor_tensor(
                        out=A[:, 2 * n:2 * n + 2, k, LO, :],
                        in0=(y_ps if k == 0 else gate_ps)[n][:, 0:HALF].rearrange("p (b q) -> p b q", b=2),
                        scalar=SCALE, in1=A[:, 2 * n:2 * n + 2, k, HI, :].bitcast(F32),
                        op0=ALU.mult, op1=ALU.subtract).then_inc(a_lo, 1)

            def write_v_lo(bb):
                dve.wait_ge(v_hi, 3 * bb + 3)
                ps = v_ps[bb]
                V_.tensor_tensor(V[:, bb, LO, :], ps[0][:, 0:D], V[:, bb, HI, :].bitcast(F32), ALU.subtract) \
                    .then_inc(v_lo, 1)
                V_.tensor_tensor(Vtail[64:64 + TAIL, bb, :], ps[1][0:TAIL, 0:D],
                                 Vtail[0:TAIL, bb, :].bitcast(F32), ALU.subtract).then_inc(v_lo, 1)

            def router_scaled():
                dve.wait_ge(gate_inv, 1)
                V_.tensor_scalar(gw_n, gw_in, gsq[:, 2:3], None, ALU.mult).then_inc(gate_scaled, 1)

            def router_lo():
                dve.wait_ge(gate_split, 1)
                V_.tensor_tensor(G[:, :, E:2 * E], y_ps[0][:, 0:KD * E].rearrange("p (k e) -> p k e", k=KD),
                                 G[:, :, 0:E].bitcast(F32), ALU.subtract).then_inc(gate_split, 1)

            def keep_mask():
                dve.wait_ge(mask_loaded, 16)
                dve.wait_ge(consts_set, 2)
                dve.wait_ge(keep_set, 2)
                for t in range(S // P):
                    ins = V_.copy_predicated(keep[:, t, :], mask_in[:, t, :], zero_keys)
                ins.then_inc(keep_set, 1)
                dve.wait_ge(keep_set, 3)

            def split_w(e):
                dve.wait_ge(w_hi, e + 1)
                V_.tensor_tensor(W[:, e, LO, :], stage[:, e % STAGES, :], W[:, e, HI, :].bitcast(F32),
                                 ALU.subtract).then_inc(w_lo, 1)

            def ln_stats(src):
                for j in range(TILES):
                    ins = V_.bn_stats(stats[:, j, :], src[:, j, :])
                ins.then_inc(bn_step, 1)

            def ln_aggr(done, b, hf, first):
                wait_apart(dve, (bn_step, upto(b, hf, 2, 1 if first else 2)))
                for j in range(TILES):
                    ins = V_.bn_aggr(meanvar[:, j, :], stats[:, j, :])
                ins.then_inc(done, 1)

            def ln_scale(src, rstd_ready, done, b, hf, q):
                if q == 0:
                    dve.wait_ge(rstd_ready, upto(b, hf, 1, 1))
                for j in (2 * q, 2 * q + 1):
                    ins = V_.tensor_scalar(xn[:, j, :], src[:, j, :], meanvar[:, j, 0:1], rstd[:, j:j + 1],
                                           ALU.subtract, ALU.mult)
                ins.then_inc(done, 1)

            def ln1_spread(b, hf):
                dve.wait_ge(x_loaded, upto(b, hf, 16, 16))
                ln_stats(xin)

            def ln1_aggr(b, hf):
                ln_aggr(ln1_stats, b, hf, True)

            def ln1_scale(b, hf, q):
                if q == 0 and not first_chunk(b, hf):
                    dve.wait_ge(t2_turned, upto(b, hf, 2, 0))
                ln_scale(xin, ln1_rstd, ln1_done, b, hf, q)

            def turned_lo(hi_done, done, b, hf, k):
                dve.wait_ge(hi_done, upto(b, hf, 2, k + 1))
                V_.tensor_tensor(xT[:, hf % 2, LO, k, :], f_ps[k][:], xT[:, hf % 2, HI, k, :].bitcast(F32),
                                 ALU.subtract).then_inc(done, 1)

            def write_t1_lo(b, hf, k):
                turned_lo(t1_hi, t1_lo, b, hf, k)

            def write_t2_lo(b, hf, k):
                turned_lo(t2_hi, t2_lo, b, hf, k)

            def mask_and_max(b, hf, q):
                if q == 0:
                    dve.wait_ge(bias_added, upto(b, hf, 1, 1))
                dve.wait_ge(scored, upto(b, hf, 2, q + 1))
                for j in (2 * q, 2 * q + 1):
                    ins = V_.tensor_tensor(att[:, j, :], f_ps[j % 2][:, KEYS:2 * KEYS], keepb[:, j, :], ALU.add)
                ins.then_inc(lo_added, 1)
                wait_apart(dve, (lo_added, upto(b, hf, 2, q + 1)))
                for j in (2 * q, 2 * q + 1):
                    ins = V_.tensor_tensor_reduce(att[:, j, :], f_ps[j % 2][:, 0:KEYS], att[:, j, :], 1.0, MASKED,
                                                  ALU.add, ALU.max, rsum[:, j:j + 1])
                ins.then_inc(maxes, 1)
                dve.wait_ge(maxes, upto(b, hf, 2, q + 1))
                V_.tensor_scalar(nmax[:, 2 * q:2 * q + 2], rsum[:, 2 * q:2 * q + 2], -1.0, None, ALU.mult) \
                    .then_inc(maxed, 1)

            def sum_reciprocal(b, hf):
                dve.wait_ge(exped, upto(b, hf, TILES, TILES))
                dve.wait_ge(maxed, upto(b, hf, 2, 2))
                V_.reciprocal(rsum, esum).then_inc(rsummed, 1)

            def write_probs_lo(b, hf, q):
                if q == 0:
                    dve.wait_ge(p_hi, upto(b, hf, 3, 1))
                    V_.tensor_tensor(xT[:, hf % 2, LO, 0, :], f_ps[0][:], xT[:, hf % 2, HI, 0, :].bitcast(F32),
                                     ALU.subtract).then_inc(p_lo, 1)
                else:
                    dve.wait_ge(p_hi, upto(b, hf, 3, 3))
                    V_.tensor_tensor(ptail[32:32 + TAIL, :], f_ps[1][0:TAIL, :], ptail[0:TAIL, :].bitcast(F32),
                                     ALU.subtract).then_inc(p_lo, 1)

            def residual(b, hf, q):
                if q == 0:
                    dve.wait_ge(rsummed, upto(b, hf, 1, 1))
                    dve.wait_ge(stored, upto(b, hf, 16, 16))
                dve.wait_ge(attended, upto(b, hf, 2, q + 1))
                for j in (2 * q, 2 * q + 1):
                    ins = V_.scalar_tensor_tensor(out=x2[:, hf % 2, j, :],
                                                  in0=f_ps[q][:, (j % 2) * D:(j % 2 + 1) * D],
                                                  scalar=rsum[:, j:j + 1], in1=xin[:, j, :],
                                                  op0=ALU.mult, op1=ALU.add)
                ins.then_inc(x2_made, 1)

            def ln2_spread(b, hf):
                dve.wait_ge(x2_made, upto(b, hf, 2, 2))
                ln_stats(x2[:, hf % 2])

            def ln2_aggr(b, hf):
                ln_aggr(ln2_stats, b, hf, False)

            def ln2_scale(b, hf, q):
                ln_scale(x2[:, hf % 2], ln2_rstd, ln2_done, b, hf, q)

            def sum_logits(b, hf):
                dve.wait_ge(z_turned, upto(b, hf, 1, 1))
                V_.tensor_reduce(z, f_ps[0][:, 0:TILES * 2 * E].rearrange("p (j t e) -> p j e t", j=TILES, t=2),
                                 AX_X, ALU.add).then_inc(z_summed, 1)

            def top_eight(b, hf):
                dve.wait_ge(tanh_z, upto(b, hf, 1, 1))
                V_.tensor_scalar(score, z, 0.5, 0.5, ALU.mult, ALU.add).then_inc(scores_set, 1)
                wait_apart(dve, (scores_set, upto(b, hf, 1, 1)))
                for j in range(TILES):
                    ins = V_.max(top8[:, j, :], score[:, j, :])
                ins.then_inc(topped, 1)
                wait_apart(dve, (topped, upto(b, hf, 1, 1)))
                for j in range(TILES):
                    V_.match_replace(rest[:, j, :], top8[:, j, :], score[:, j, :], 0.0).then_inc(rest_set, 1)
                V_.tensor_reduce(ssum, top8[:], AX_X, ALU.add).then_inc(rest_set, 1)

            def weights(b, hf):
                dve.wait_ge(rest_set, upto(b, hf, TILES + 1, TILES + 1))
                V_.tensor_tensor(cw, score, rest, ALU.subtract).then_inc(picked, 1)
                V_.reciprocal(srec, ssum).then_inc(picked, 1)
                dve.wait_ge(picked, upto(b, hf, 2, 2))
                for j in range(TILES):
                    ins = V_.tensor_scalar(cw[:, j, :], cw[:, j, :], srec[:, j:j + 1], 0.5, ALU.mult, ALU.mult)
                ins.then_inc(combined, 1)

            def silu_up(b, hf, e):
                hf, e = nxt(hf, e)
                i = slot(hf, e)
                dve.wait_ge(tanh_done, upto(b, hf, NE, e + 1))
                V_.scalar_tensor_tensor(out=ew[:, i, :], in0=ew[:, i, :], scalar=1.0, in1=gate_ps[i][:],
                                        op0=ALU.add, op1=ALU.mult).then_inc(silu_done, 1)
                dve.wait_ge(silu_done, upto(b, hf, NE, e + 1 + FREE))
                dve.wait_ge(up_done, upto(b, hf, NE, e + 1))
                V_.tensor_tensor(ew[:, i, :], ew[:, i, :], up_ps[i][:], ALU.mult).then_inc(prod_done, 1)

            def hidden_lo(b, hf, e):
                hf, e = nxt(hf, e)
                i = slot(hf, e)
                dve.wait_ge(h_hi, upto(b, hf, NE, e + 1 + FREE))
                V_.tensor_tensor(hs[:, i, LO, :], h[:, i, :], hs[:, i, HI, :].bitcast(F32), ALU.subtract) \
                    .then_inc(h_lo, 1)

            def add_y(b, hf):
                for q in range(2):
                    if q == 0:
                        dve.wait_ge(y_half, upto(b, hf, 1, 1))
                    else:
                        dve.wait_ge(down_done, upto(b, hf, NE, NE + FREE))
                    v = x2[:, hf, 2 * q:2 * q + 2, :].rearrange("p j d -> p (j d)")
                    V_.tensor_tensor(v, v, y_ps[q][:], ALU.add).then_inc(y_added, 1)

            def front(at, b, hf):
                if due(DVE_AT, "ln1_stats", at):
                    ln1_spread(b, hf)
                if due(DVE_AT, "ln1_aggr", at):
                    ln1_aggr(b, hf)
                for part in due(DVE_AT, "ln1_scale", at):
                    ln1_scale(b, hf, part)
                for part in due(DVE_AT, "t1_lo", at):
                    write_t1_lo(b, hf, part)
                for part in due(DVE_AT, "maxes", at):
                    mask_and_max(b, hf, part)
                if due(DVE_AT, "sum_reciprocal", at):
                    sum_reciprocal(b, hf)
                for part in due(DVE_AT, "probs_lo", at):
                    write_probs_lo(b, hf, part)
                for part in due(DVE_AT, "residual", at):
                    residual(b, hf, part)
                if due(DVE_AT, "ln2_stats", at):
                    ln2_spread(b, hf)
                if due(DVE_AT, "ln2_aggr", at):
                    ln2_aggr(b, hf)
                for part in due(DVE_AT, "ln2_scale", at):
                    ln2_scale(b, hf, part)
                for part in due(DVE_AT, "t2_lo", at):
                    write_t2_lo(b, hf, part)
                if due(DVE_AT, "sum_logits", at):
                    sum_logits(b, hf)
                if due(DVE_AT, "top_eight", at):
                    top_eight(b, hf)
                if due(DVE_AT, "weights", at):
                    weights(b, hf)

            def chunk(b, hf, ahead, last):
                for s in range(NE):
                    if s + 2 < NE or not last:
                        silu_up(b, hf, s + 2)
                    if ahead:
                        front(s, b, hf + 1)
                    if s + 1 < NE or not last:
                        hidden_lo(b, hf, s + 1)
                    if ahead:
                        front(s + .5, b, hf + 1)
                add_y(b, hf)

            for s_ in (silu_done, prod_done, h_lo):
                dve.sem_inc(s_, FREE)
            dve.sem_inc(y_added, FREE)
            read_ctx()
            write_wqT()
            ln1_spread(0, 0)
            ln1_aggr(0, 0)
            ln1_scale(0, 0, 0)
            ln1_scale(0, 0, 1)
            pads()
            write_t1_lo(0, 0, 0)
            write_t1_lo(0, 0, 1)
            keep_mask()
            for e in SPLITS["A0"]:
                split_w(e)
            write_a_lo(0)
            for e in SPLITS["A1"]:
                split_w(e)
            write_a_lo(1)
            write_v_lo(0)
            for e in SPLITS["exps"]:
                split_w(e)
            mask_and_max(0, 0, 0)
            write_v_lo(1)
            mask_and_max(0, 0, 1)
            sum_reciprocal(0, 0)
            write_v_lo(2)
            router_scaled()
            for e in SPLITS["probs"]:
                split_w(e)
            dve.wait_ge(pads_set, 2)
            write_probs_lo(0, 0, 0)
            write_probs_lo(0, 0, 1)
            residual(0, 0, 0)
            residual(0, 0, 1)
            ln2_spread(0, 0)
            ln2_aggr(0, 0)
            for e in SPLITS["V3"]:
                split_w(e)
            write_v_lo(3)
            router_lo()
            ln2_scale(0, 0, 0)
            ln2_scale(0, 0, 1)
            for e in SPLITS["t2_hi"]:
                split_w(e)
            write_t2_lo(0, 0, 0)
            write_t2_lo(0, 0, 1)
            for e in SPLITS["tanh_scores"]:
                split_w(e)
            sum_logits(0, 0)
            top_eight(0, 0)
            weights(0, 0)
            silu_up(0, 0, 0)
            for e in SPLITS["tanh1"]:
                split_w(e)
            silu_up(0, 0, 1)
            for e in SPLITS["hidden"]:
                split_w(e)
            hidden_lo(0, 0, 0)
            for e in SPLITS["end"]:
                split_w(e)
            with dve.Fori(0, B - 1) as b:
                chunk(b, 0, True, False)
                chunk(b, 1, True, False)
            chunk(B - 1, 0, True, False)
            chunk(B - 1, 1, False, True)

        @block.gpsimd
        def _(pool):
            pg = nc.gpsimd

            def setup():
                pg.memset(ident[:], 0.0).then_inc(pool_step, 1)
                pg.memset(minus_half[:], -0.5)
                pg.memset(ones1[:], 1.0)
                pool.wait_ge(pool_step, 1)
                pg.affine_select(out=ident[:], in_=ident[:], compare_op=ALU.not_equal, fill=1.0, base=0,
                                 pattern=[[-1, P]], channel_multiplier=1).then_inc(consts_set, 1)

            def zeros():
                pg.memset(zero_keys, 0.0).then_inc(keep_set, 1)
                pg.memset(keep[:], MASKED).then_inc(keep_set, 1)
                pg.memset(Vtail[:].bitcast(U32), 0).then_inc(pads_set, 1)
                pg.memset(ptail[:].bitcast(U32), 0).then_inc(pads_set, 1)

            def gate_norm():
                pool.wait_ge(gate_summed, 1)
                pg.tensor_scalar(gsq[:, 1:2], gsq[:, 0:1], 1.0, NORM_EPS ** 2, ALU.mult, ALU.max) \
                    .then_inc(pool_step, 1)
                pool.wait_ge(pool_step, 2)
                pg.tensor_tensor(gsq[:, 2:3], gsq[:, 1:2], minus_half[0:E, 0:1], ALU.pow).then_inc(gate_inv, 1)

            def inverse_std(stats_ready, done, b, hf):
                wait_apart(pool, (stats_ready, upto(b, hf, 1, 1)))
                pg.tensor_scalar(var_eps, meanvar[:, :, 1], LN_EPS, 1.0, ALU.add, ALU.mult).then_inc(std_step, 1)
                first = stats_ready is ln1_stats
                pool.wait_ge(std_step, upto(b, hf, 2, 1 if first else 2))
                pg.tensor_tensor(rstd, var_eps, minus_half[:], ALU.pow).then_inc(done, 1)

            def add_bias(b, hf):
                if first_chunk(b, hf):
                    pool.wait_ge(keep_set, 3)
                    pool.wait_ge(brow_scaled, 2)
                else:
                    pool.wait_ge(maxes, upto(b, hf, 2, 0))
                bi = b + hf // 2
                pg.tensor_tensor(keepb[:], keep[:, (hf % 2) * TILES:(hf % 2 + 1) * TILES, :],
                                 brow[:, bass.ds(bi * KEYS, KEYS)].unsqueeze(1).broadcast_to([P, TILES, KEYS]),
                                 ALU.add).then_inc(bias_added, 1)

            def ln1_std(b, hf):
                inverse_std(ln1_stats, ln1_rstd, b, hf)

            def ln2_std(b, hf):
                inverse_std(ln2_stats, ln2_rstd, b, hf)

            def inverse_norm(b, hf):
                pool.wait_ge(ln2_rstd, upto(b, hf, 1, 1))
                pg.tensor_tensor(rsq, rstd, rstd, ALU.mult).then_inc(norm_step, 1)
                pool.wait_ge(norm_step, upto(b, hf, 3, 1))
                pg.tensor_tensor(nsq, rsq, meanvar[:, :, 1], ALU.mult).then_inc(norm_step, 1)
                wait_apart(pool, (norm_step, upto(b, hf, 3, 2)))
                pg.tensor_scalar(nsq, nsq, 4.0 * D, 4.0 * NORM_EPS ** 2, ALU.mult, ALU.max).then_inc(norm_step, 1)
                pool.wait_ge(norm_step, upto(b, hf, 3, 3))
                pg.tensor_tensor(inorm, nsq, minus_half[:], ALU.pow).then_inc(inv_norms, 1)

            def weighted(b, hf, e):
                hf, e = nxt(hf, e)
                i = slot(hf, e)
                if e == 0:
                    wait_apart(pool, (prod_done, upto(b, hf, NE, 1 + FREE)), (h_hi, upto(b, hf, NE, FREE - 1)),
                               (h_lo, upto(b, hf, NE, FREE - 1)))
                    pg.tensor_scalar(h[:, i, :], ew[:, i, :], 0.5, 1.0, ALU.mult, ALU.mult).then_inc(h_done, 1)
                else:
                    pool.wait_ge(prod_done, upto(b, hf, NE, e + 1 + FREE))
                    pool.wait_ge(h_hi, upto(b, hf, NE, e - 1 + FREE))
                    pool.wait_ge(h_lo, upto(b, hf, NE, e - 1 + FREE))
                    pair = (e - 1) // 2
                    pool.wait_ge(cb_loaded[pair % PLACES], upto(b, hf, 32, 16 * (pair // PLACES + 1)))
                    pg.tensor_tensor(h[:, i, :], ew[:, i, :], cb[:, pair % PLACES, (e - 1) % 2, :], ALU.mult) \
                        .then_inc(h_done, 1)

            def front(at, b, hf):
                if due(POOL_AT, "add_bias", at):
                    add_bias(b, hf)
                if due(POOL_AT, "ln1_std", at):
                    ln1_std(b, hf)
                if due(POOL_AT, "ln2_std", at):
                    ln2_std(b, hf)
                if due(POOL_AT, "inverse_norm", at):
                    inverse_norm(b, hf)

            def chunk(b, hf, ahead, last):
                for s in range(NE):
                    if s + 1 < NE or not last:
                        weighted(b, hf, s + 1)
                    if ahead:
                        front(s + .5, b, hf + 1)

            pool.sem_inc(h_done, FREE)
            setup()
            zeros()
            ln1_std(0, 0)
            add_bias(0, 0)
            gate_norm()
            ln2_std(0, 0)
            inverse_norm(0, 0)
            weighted(0, 0, 0)
            with pool.Fori(0, B - 1) as b:
                chunk(b, 0, True, False)
                chunk(b, 1, True, False)
            chunk(B - 1, 0, True, False)
            chunk(B - 1, 1, False, True)


_INS = ['x', 'ctx_1024', 'mask_SxS2_bk0', 'L0_xattn_Wq', 'L0_xattn_bq', 'L0_xattn_Wk', 'L0_xattn_bk',
        'L0_xattn_Wv', 'L0_xattn_bv', 'L0_ffn_gate_w', 'L0_ffn_w_gate', 'L0_ffn_w_up', 'L0_ffn_w_down',
        'L0_ffn_sw_gate', 'L0_ffn_sw_up', 'L0_ffn_sw_down']


def kernel(**inputs):
    import numpy as _np
    import concourse.bacc as _bacc
    from concourse.bass_utils import run_bass_kernel_spmd as _run

    nc = _bacc.Bacc("TRN2", target_bir_lowering=False, num_devices=1, dynamic_dma_scratch_size=1024)
    arrays, args = {}, []
    for name in _INS:
        a = _np.ascontiguousarray(inputs[name])
        arrays[f"in_{name}_dram"] = a
        args.append(nc.dram_tensor(f"in_{name}_dram", a.shape, mybir.dt.from_np(a.dtype), kind="ExternalInput").ap())
    out = nc.dram_tensor("out_0_dram", arrays["in_x_dram"].shape, F32, kind="ExternalOutput").ap()
    xattn_moe_kernel(nc, *args, out)
    r = _run(nc, [arrays], core_ids=[0])
    return r.results[0]["out_0_dram"]
```
